# Optimizing a Trainium2 kernel written in Bass

```python
import numpy as np
import jax
import jax.numpy as jnp

def _softmax(x, axis=-1):
    return jax.nn.softmax(x, axis=axis)

def _gelu(x):
    return jax.nn.gelu(x, approximate=True)

def _silu(x):
    return jax.nn.silu(x)

def _sigmoid(x):
    return jax.nn.sigmoid(x)

def _layernorm(x, axis=-1, eps=1e-05):
    m = jnp.mean(x, axis=axis, keepdims=True)
    v = jnp.var(x, axis=axis, keepdims=True)
    return (x - m) / jnp.sqrt(v + eps)

def _scatter_add(tgt, idx, src, axis=0):
    return tgt.at[idx].add(src)

def _segment_sum(src, seg, n):
    return jax.ops.segment_sum(src, seg, n)
kernel_name = 'mk_macaron_d2_jaxref_r8_925d19'

def setup_inputs(seed: int=0):
    np.random.seed(seed)
    _w = jnp.asarray

    def _L0_attn_setup():
        import jax, jax.numpy as jnp
        import numpy as np
        from math import sqrt
        D_MODEL = 128
        NUM_HEADS = 16
        D_HEAD = D_MODEL // NUM_HEADS
        THETA = 10000.0

        def _rope(x, freqs):
            xr = x[..., ::2]
            xi = x[..., 1::2]
            cos = jnp.cos(freqs)
            sin = jnp.sin(freqs)
            yr = xr * cos - xi * sin
            yi = xr * sin + xi * cos
            return jnp.stack([yr, yi], axis=-1).reshape(x.shape)
        key = jax.random.key(seed)
        k1, k2, k3 = jax.random.split(key, 3)
        X = jax.random.normal(k1, (4, 256, D_MODEL), dtype=jnp.float32)
        std_kqv = sqrt(2.0 / (D_MODEL + 3 * D_MODEL))
        W_KQV = std_kqv * jax.random.truncated_normal(k2, -3.0, 3.0, (3 * D_MODEL, D_MODEL), dtype=jnp.float32)
        std_o = sqrt(2.0 / (D_MODEL + D_MODEL))
        W_O = std_o * jax.random.truncated_normal(k3, -3.0, 3.0, (D_MODEL, D_MODEL), dtype=jnp.float32)
        return {'X': X, 'W_KQV': W_KQV, 'W_O': W_O}
    _L0_attn_in = _L0_attn_setup()

    def _L0_ffn_setup():
        import jax, jax.numpy as jnp
        import numpy as np
        B, S, IN, OUT = (4, 1024, 128, 128)
        EPS = 1e-06

        def _xla_quantized_matmul(x2d, weight_q, weight_scale):
            amax = jnp.max(jnp.abs(x2d), axis=-1, keepdims=True)
            x_scale = jnp.maximum(amax, EPS) / 127.0
            x_q = jnp.clip(jnp.round(x2d / x_scale), -128, 127).astype(jnp.int8)
            acc = jax.lax.dot_general(x_q, weight_q, (((1,), (1,)), ((), ())), preferred_element_type=jnp.int32)
            return acc.astype(jnp.float32) * x_scale * weight_scale[None, :]
        key = jax.random.key(seed)
        k1, k2, k3, k4 = jax.random.split(key, 4)
        x = jax.random.normal(k1, (B, S, IN), dtype=jnp.float32)
        weight_q = jax.random.randint(k2, (OUT, IN), -128, 128, dtype=jnp.int32).astype(jnp.int8)
        weight_scale = jax.random.uniform(k3, (OUT,), dtype=jnp.float32, minval=0.001, maxval=0.01)
        bias = jax.random.normal(k4, (OUT,), dtype=jnp.float32) * 0.01
        return {'x': x, 'weight_q': weight_q, 'weight_scale': weight_scale, 'bias': bias}
    _L0_ffn_in = _L0_ffn_setup()

    def _L1_attn_setup():
        import jax, jax.numpy as jnp
        import numpy as np
        import math
        B, T, C = (2, 256, 128)
        H, DK, DV = (16, 64, 64)
        key = jax.random.key(seed)
        ks = jax.random.split(key, 5)
        x = jax.random.normal(ks[0], (B, T, C), dtype=jnp.float32)
        w_q = jax.random.normal(ks[1], (H, DK, C), dtype=jnp.float32) / math.sqrt(C)
        w_k = jax.random.normal(ks[2], (H, DK, C), dtype=jnp.float32) / math.sqrt(C)
        w_v = jax.random.normal(ks[3], (H, DV, C), dtype=jnp.float32) / math.sqrt(C)
        w_o = jax.random.normal(ks[4], (H * DV, C), dtype=jnp.float32) / math.sqrt(C)
        return {'x': x, 'w_q': w_q, 'w_k': w_k, 'w_v': w_v, 'w_o': w_o}
    _L1_attn_in = _L1_attn_setup()

    def _L1_ffn_setup():
        import jax, jax.numpy as jnp
        import numpy as np
        DIM = 128
        HIDDEN = 384
        SCALE = 1.0 / 127.0

        def _dequant(w_int, dtype):
            return w_int.astype(dtype) * jnp.asarray(SCALE, dtype)
        key = jax.random.key(seed)
        k_x, k_g, k_u, k_d = jax.random.split(key, 4)
        x = jax.random.normal(k_x, (4, 256, DIM), dtype=jnp.float32)
        w_gate = jax.random.randint(k_g, (HIDDEN, DIM), -127, 128, dtype=jnp.int32)
        w_up = jax.random.randint(k_u, (HIDDEN, DIM), -127, 128, dtype=jnp.int32)
        w_down = jax.random.randint(k_d, (DIM, HIDDEN), -127, 128, dtype=jnp.int32)
        return {'x': x, 'w_gate': w_gate, 'w_up': w_up, 'w_down': w_down}
    _L1_ffn_in = _L1_ffn_setup()
    _d = {'L0_attn_X': _L0_attn_in['X'], 'L0_attn_W_KQV': _L0_attn_in['W_KQV'], 'L0_attn_W_O': _L0_attn_in['W_O'], 'L0_ffn_weight_q': _L0_ffn_in['weight_q'], 'L0_ffn_weight_scale': _L0_ffn_in['weight_scale'], 'L0_ffn_bias': _L0_ffn_in['bias'], 'L1_attn_w_q': _L1_attn_in['w_q'], 'L1_attn_w_k': _L1_attn_in['w_k'], 'L1_attn_w_v': _L1_attn_in['w_v'], 'L1_attn_w_o': _L1_attn_in['w_o'], 'L1_ffn_w_gate': _L1_ffn_in['w_gate'], 'L1_ffn_w_up': _L1_ffn_in['w_up'], 'L1_ffn_w_down': _L1_ffn_in['w_down']}
    _x0 = _d['L0_attn_X']
    _d['L0_attn_X'] = jax.random.normal(jax.random.fold_in(jax.random.key(seed), 1), (2, 1024, 128), dtype=_x0.dtype)
    del _x0
    return _d

def reference(L0_attn_X, L0_attn_W_KQV, L0_attn_W_O, L0_ffn_weight_q, L0_ffn_weight_scale, L0_ffn_bias, L1_attn_w_q, L1_attn_w_k, L1_attn_w_v, L1_attn_w_o, L1_ffn_w_gate, L1_ffn_w_up, L1_ffn_w_down):

    def _L0_attn_ref(X, W_KQV, W_O):
        import jax, jax.numpy as jnp
        import numpy as np
        from math import sqrt
        D_MODEL = 128
        NUM_HEADS = 16
        D_HEAD = D_MODEL // NUM_HEADS
        THETA = 10000.0

        def _rope(x, freqs):
            xr = x[..., ::2]
            xi = x[..., 1::2]
            cos = jnp.cos(freqs)
            sin = jnp.sin(freqs)
            yr = xr * cos - xi * sin
            yi = xr * sin + xi * cos
            return jnp.stack([yr, yi], axis=-1).reshape(x.shape)
        B, S, D = X.shape
        H, d = (NUM_HEADS, D_HEAD)
        KQV = jnp.einsum('bsd,ed->bse', X, W_KQV)
        K, Q, V = jnp.split(KQV, [D, 2 * D], axis=-1)

        def to_heads(t):
            return t.reshape(B, S, H, d).transpose(0, 2, 1, 3)
        K, Q, V = (to_heads(K), to_heads(Q), to_heads(V))
        inv_freq = 1.0 / THETA ** (jnp.arange(0, d, 2, dtype=jnp.float32) / d)
        pos = jnp.arange(S, dtype=jnp.float32)
        freqs = pos[:, None] * inv_freq[None, :]
        Q = _rope(Q, freqs)
        K = _rope(K, freqs)
        scores = jnp.einsum('bhqd,bhkd->bhqk', Q, K) / sqrt(d)
        causal = jnp.triu(jnp.ones((S, S), dtype=bool), k=1)
        scores = jnp.where(causal, -jnp.inf, scores)
        probs = jax.nn.softmax(scores, axis=-1)
        heads = jnp.einsum('bhqk,bhkd->bhqd', probs, V)
        acts = heads.transpose(0, 2, 1, 3).reshape(B, S, D)
        return jnp.einsum('bsd,ed->bse', acts, W_O)

    def _L0_ffn_ref(x, weight_q, weight_scale, bias):
        import jax, jax.numpy as jnp
        import numpy as np
        B, S, IN, OUT = (4, 1024, 128, 128)
        EPS = 1e-06

        def _xla_quantized_matmul(x2d, weight_q, weight_scale):
            amax = jnp.max(jnp.abs(x2d), axis=-1, keepdims=True)
            x_scale = jnp.maximum(amax, EPS) / 127.0
            x_q = jnp.clip(jnp.round(x2d / x_scale), -128, 127).astype(jnp.int8)
            acc = jax.lax.dot_general(x_q, weight_q, (((1,), (1,)), ((), ())), preferred_element_type=jnp.int32)
            return acc.astype(jnp.float32) * x_scale * weight_scale[None, :]
        orig_shape = x.shape
        x2d = x.reshape(-1, orig_shape[-1])
        out = _xla_quantized_matmul(x2d, weight_q, weight_scale)
        out = out.reshape(*orig_shape[:-1], out.shape[-1])
        out = out + bias
        return out

    def _L1_attn_ref(x, w_q, w_k, w_v, w_o):
        import jax, jax.numpy as jnp
        import numpy as np
        import math
        B, T, C = (2, 256, 128)
        H, DK, DV = (16, 64, 64)
        dk = w_q.shape[1]
        q = jnp.einsum('ntc,hdc->nhtd', x, w_q)
        k = jnp.einsum('ntc,hdc->nhtd', x, w_k)
        v = jnp.einsum('ntc,hdc->nhtd', x, w_v)
        a = jnp.einsum('nhtd,nhsd->nhts', q, k) / jnp.sqrt(jnp.asarray(dk, x.dtype))
        t = a.shape[-1]
        mask = jnp.arange(t)[:, None] < jnp.arange(t)[None, :]
        a = jnp.where(mask[None, None], jnp.asarray(-jnp.inf, a.dtype), a)
        a = jax.nn.softmax(a, axis=-1)
        y = jnp.einsum('nhts,nhsd->nthd', a, v)
        y = y.reshape(y.shape[0], y.shape[1], -1)
        return y @ w_o

    def _L1_ffn_ref(x, w_gate, w_up, w_down):
        import jax, jax.numpy as jnp
        import numpy as np
        DIM = 128
        HIDDEN = 384
        SCALE = 1.0 / 127.0

        def _dequant(w_int, dtype):
            return w_int.astype(dtype) * jnp.asarray(SCALE, dtype)
        wg = _dequant(w_gate, x.dtype)
        wu = _dequant(w_up, x.dtype)
        wd = _dequant(w_down, x.dtype)
        gate = jnp.einsum('bsd,hd->bsh', x, wg)
        up = jnp.einsum('bsd,hd->bsh', x, wu)
        h = jax.nn.silu(gate) * up
        return jnp.einsum('bsh,dh->bsd', h, wd)
    x = L0_attn_X
    x = x + 0.5 * _L0_ffn_ref(_layernorm(x, axis=-1), L0_ffn_weight_q, L0_ffn_weight_scale, L0_ffn_bias)
    x = x + _L0_attn_ref(_layernorm(x, axis=-1), L0_attn_W_KQV, L0_attn_W_O)
    x = x + 0.5 * _L0_ffn_ref(_layernorm(x, axis=-1), L0_ffn_weight_q, L0_ffn_weight_scale, L0_ffn_bias)
    x = x + 0.5 * _L1_ffn_ref(_layernorm(x, axis=-1), L1_ffn_w_gate, L1_ffn_w_up, L1_ffn_w_down)
    x = x + _L1_attn_ref(_layernorm(x, axis=-1), L1_attn_w_q, L1_attn_w_k, L1_attn_w_v, L1_attn_w_o)
    x = x + 0.5 * _L1_ffn_ref(_layernorm(x, axis=-1), L1_ffn_w_gate, L1_ffn_w_up, L1_ffn_w_down)
    return x

_drawn_inputs = setup_inputs


def setup_inputs(seed=0):
    import zlib

    import numpy as np

    out = dict(_drawn_inputs(seed))
    spreads = {}
    factors = {'L0_ffn_bias': 7.92,
     'L1_attn_w_q': 8.0,
     'L1_attn_w_k': 8.0,
     'L1_attn_w_v': 8.0,
     'L1_attn_w_o': 8.0}
    for name, (base, spread) in spreads.items():
        noise = np.random.default_rng([zlib.crc32(name.encode()), seed]).standard_normal(out[name].shape)
        drawn = base * np.exp(spread * noise) if base else spread * noise
        out[name] = jnp.asarray(drawn.astype(out[name].dtype))
    for name, factor in factors.items():
        out[name] = (out[name] * factor).astype(out[name].dtype)
    return out
```

```python
from contextlib import ExitStack

import concourse.bass as bass
from concourse import mybir

ALU = mybir.AluOpType
ACT = mybir.ActivationFunctionType
AX = mybir.AxisListType
F32 = mybir.dt.float32
BF16 = mybir.dt.bfloat16
F16 = mybir.dt.float16
I32 = mybir.dt.int32
I64 = mybir.dt.int64

P = 128
B = 2
S = 1024
T = S // P
H = 16
D0 = P // H
D1 = 64
HID = 384
HC = HID // P
SLOTS = 8
GH = 4
G = B * H // GH
GB = H // GH
SHIFT_TOP, SHIFT_LOW = 2.0**14, 2.0**3
QK_BOUND = 4096.0
VW = 66
NP = H // 2
LN_EPS = 1e-5
Q_EPS = 1e-6
MAGIC = 1.5 * 2.0**23
SCALE0 = float(D0) ** -0.5
SCALE1 = float(D1) ** -0.5
W_SCALE = 1.0 / 127.0
RING = 3

Q_PARTS = (0, 0, 1, 1, 0, 2)
K_PARTS = (0, 1, 0, 1, 2, 0)
SHIFT_SLOT = 6


def plan_units():
    units = []

    def int_ffn(s):
        for b in range(B):
            units.append((("turn", s, b), "A"))
            units.append((("mm", s, b), "V"))

    def gated_ffn(s):
        for b in range(B):
            units.append((("turn", s, b), "A"))
            for c in range(HC):
                units.append((("up", s, b, c), "AV"))
            units.append((("mm", s, b), "V"))

    int_ffn(0)
    for b in range(B):
        units.append((("turn", 1, b), "A"))
        for half in range(2):
            units.append((("qkv", b, half), "AV"))
    for b in range(B):
        units.append((("acts", b), "A"))
        units.append((("mm", 1, b), "V"))
    units.append((("wscale",), "V"))
    int_ffn(2)
    gated_ffn(3)
    for b in range(B):
        units.append((("turn", 4, b), "A"))
    for b in range(B):
        units.append((("mm", 4, b), "V"))
    gated_ffn(5)
    return units


UNITS = plan_units()
UNIT_AT = {key: n for n, (key, _) in enumerate(UNITS)}


def filled(key):
    return UNIT_AT[key] + 1


def read_by(engine, n):
    return sum(engine in who for _, who in UNITS[: n + 1])


def grouped(widths):
    steps = []
    for t, w in widths:
        n = 1 if w > 512 else 2 if w > 256 else 4
        steps += [(t, j, n) for j in range(0, GH, n)]
    return steps


MAX_STEPS = grouped([(t, (t + 1) * P) for t in range(T)])
EXP_STEPS = grouped([(t, (T - t) * P) for t in range(T)])


def group_steps(exps, maxes, turn_next, turn_after):
    steps = []
    for n in range(len(EXP_STEPS)):
        if exps:
            steps.append(("exp", 0, EXP_STEPS[n], "A"))
        if maxes:
            steps.append(("max", 1, MAX_STEPS[n], "V"))
    if turn_next:
        steps.append(("shifted_q", 1, None, "V"))
    if exps:
        steps.append(("heads", 0, None, "V"))
    if turn_after:
        steps.append(("k", 1, None, "A"))
        steps.append(("q", 1, None, "V"))
    return steps


def pair_steps(exps, maxes, project):
    steps = []
    for h in range(2):
        for t in range(T):
            if exps:
                steps.append(("exp", h, t, "A"))
            if maxes and (h, t) == (1, 1):
                steps.append(("shift", 0, None, "A"))
            if maxes:
                steps.append(("max", h, t, "V"))
    if project:
        steps += [("proj_q", 2, None, "V"), ("proj_k", 2, None, "V")]
    if maxes:
        steps.insert(len(steps) if exps else len(steps) - 2, ("shift", 1, None, "A"))
    if project:
        steps.append(("proj_v", 2, None, "V"))
    if exps:
        steps += [("yT", 0, None, "V"), ("yT", 1, None, "V")]
    return steps


class Turn:

    def __init__(self, steps, times=1, after=None):
        self.steps, self.times = steps, times
        self.before = after
        self.n0 = after.n0 + after.times * len(after.steps) if after else 0
        self.c0 = {e: (after.c0[e] + after.times * after.reads(e)) if after else 0 for e in "AV"}
        assert self.n0 % RING == 0 and (times == 1 or len(steps) % RING == 0)

    def reads(self, e, upto=None):
        return sum(s[-1] == e for s in self.steps[:upto])

    def filled(self, k, i):
        return self.n0 + k + 1 + i * len(self.steps)

    def read(self, e, k, i):
        return self.c0[e] + self.reads(e, k + 1) + i * self.reads(e)

    def bank(self, k):
        return 2 * ((self.n0 + k) % RING)

    def freed(self, k, i):
        if k >= RING:
            e = self.steps[k - RING][-1]
            return e, self.read(e, k - RING, i)
        back = RING - k
        last = self.before or self
        if self.before is None:
            return None
        if self.times > 1:
            assert [s[-1] for s in self.steps[-RING:]] == [s[-1] for s in last.steps[-RING:]]
        e = last.steps[-back][-1]
        later = sum(s[-1] == e for s in last.steps[len(last.steps) - back + 1 :])
        return e, self.c0[e] - later + i * self.reads(e)


GROUP_FIRST = Turn(
    [("k", 0, None, "A"), ("q", 0, None, "V")]
    + [("max", 0, m, "V") for m in MAX_STEPS]
    + [("shifted_q", 0, None, "V"), ("k", 1, None, "A"), ("q", 1, None, "V")]
)
GROUP_LOOP = Turn(2 * group_steps(True, True, True, True), (G - 2) // 2, GROUP_FIRST)
GROUP_LAST = Turn(
    group_steps(True, True, True, False) + group_steps(True, False, False, False), 1, GROUP_LOOP
)
PROJECT = [("proj_q", 1, None, "V"), ("proj_k", 1, None, "V"), ("proj_v", 1, None, "V")]


def pair_turns():
    turns, after = [], GROUP_LAST
    for _ in range(B):
        first = Turn(PROJECT + pair_steps(False, True, True), 1, after)
        loop = Turn(2 * pair_steps(True, True, True), (NP - 2) // 2, first)
        last = Turn(pair_steps(True, True, False) + pair_steps(True, False, False), 1, loop)
        turns.append((first, loop, last))
        after = last
    return turns


PAIR_TURNS = pair_turns()


def macaron_block_kernel(nc, x, w_kqv, w_o0, w_int, w_scale, bias, w_q, w_k, w_v, w_o1, w_gate, w_up,
                         w_down, ident, mask_q, mask_k, head_mask, rope_cos, rope_sin, out):
    ctx = ExitStack()
    with ctx:
        def sb(name, shape, dt=F32):
            return ctx.enter_context(nc.sbuf_tensor(name, shape, dt))

        def sem(name):
            return ctx.enter_context(nc.semaphore(name))

        X = sb("X", [P, B, T, P])
        work = sb("work", [P, 2, B, T, P])
        D = work[:, 0]
        W = work[:, 1]
        XQ = sb("XQ", [P, B, T, P], BF16)
        XQT = sb("XQT", [P, B, S], BF16)
        XT = sb("XT", [P, B, S])
        ffn_h = sb("ffn_h", [P, HC, S])
        big = sb("big", [P, 16384])
        Pr = sb("Pr", [P, 2, GH, S])
        ffn_g = Pr[:, 0, 2:4, :]
        V0 = sb("V0", [P, G, T, GH * D0])
        VS = sb("VS", [P, 2, T, GH, 32])
        OT = sb("OT", [P, S])
        acts = sb("acts", [P, G, T, GH * D0])
        stats = sb("stats", [P, 16, B, T])
        mx0 = sb("mx0", [P, T, GH])
        mr0 = sb("mr0", [P, 2, T, GH])
        rs0 = sb("rs0", [P, T, GH])
        mx1 = sb("mx1", [P, 2, T])
        sh1 = sb("sh1", [P, 2, T, 2], F16)
        rs1 = sb("rs1", [P, 2, T])
        wmax = sb("wmax", [P, 2])
        wsum = sb("wsum", [P, 2])
        qk_scale = sb("qk_scale", [P, 2])
        exp_scale = sb("exp_scale", [P, 1])
        wkqv_s = sb("wkqv_s", [P, 3 * P])
        wo0_s = sb("wo0_s", [P, P])
        wint_s = sb("wint_s", [P, P], BF16)
        wsc_s = sb("wsc_s", [P, P])
        bias_s = sb("bias_s", [P, P])
        wqkv1 = sb("wqkv1", [P, 3, H * D1])
        wo1_s = sb("wo1_s", [P, NP, P])
        wg_s = sb("wg_s", [P, 2, HID])
        wd_s = sb("wd_s", [P, HC, P])
        id_s = sb("id_s", [P, P])
        idb_s = sb("idb_s", [P, P], BF16)
        idh_s = sb("idh_s", [P, P], F16)
        ones_s = sb("ones_s", [P, P])
        mq_s = sb("mq_s", [P, P], BF16)
        mk_s = sb("mk_s", [P, P], BF16)
        hm_s = sb("hm_s", [P, 2])

        bigb = big[:, :].bitcast(BF16)
        Qs = bigb[:, 0:16384].rearrange("p (n t s c) -> p n t s c", n=B * NP, t=T, s=SLOTS)
        Ks = bigb[:, 16384:32768].rearrange("p (n t s c) -> p n t s c", n=B * NP, t=T, s=SLOTS)
        KT = work[:, :, :, :, :].rearrange("p w b t c -> p (w b t c)").bitcast(BF16).rearrange(
            "p (r h s) -> p r h s", r=2, h=GH)
        QT = ffn_h[:, 0].bitcast(BF16).rearrange("p (n s) -> p n s", n=2)
        QmT = ffn_h[:, 1].bitcast(BF16).rearrange("p (n s) -> p n s", n=2)
        bigh = big[:, :].bitcast(F16)
        QK = bigh[:, 0:16384].rearrange("p (m r h s) -> p m r h s", m=4, r=2, h=2)
        Q1, K1, Q2, K2 = (QK[:, m] for m in range(4))
        YT = big[:, 8192:16384].rearrange("p (n s) -> p n s", n=NP)
        Pr1 = Pr[:, 0, 0:2, :]
        VA = Pr[:, 1, :, :].rearrange("p a s -> p (a s)")[:, 0:2 * T * 2 * VW].rearrange(
            "p (r t h c) -> p r t h c", r=2, t=T, h=2)
        Y1 = OT[:, :].rearrange("p (t c) -> p t c", t=T)
        ws1 = sb("ws1", [P, 2, 2, P])
        prf = Pr[:, :, :, :].rearrange("p r h s -> p (r h s)")
        cosT = prf[:, 0:2048].rearrange("p (t c) -> p t c", t=T)
        sinT = prf[:, 2048:4096].rearrange("p (t c) -> p t c", t=T)
        R = prf[:, 4096:5120].rearrange("p (t c) -> p t c", t=4)
        R2 = prf[:, 5120:6144].rearrange("p (t c) -> p t c", t=4)
        raw_gu = ffn_h[:, 0, 0:2 * HID].bitcast(I32).rearrange("p (a c) -> p a c", a=2)
        raw_masks = ffn_h[:, 2, 2 * P:4 * P].rearrange("p (a c) -> p a c", a=2)
        raw_int = ffn_h[:, 2, 0:2 * P].bitcast(I64)
        raw_d = ffn_h[:, 1, 0:HID].bitcast(I32).rearrange("p (a c) -> p a c", a=HC)

        ps = ctx.enter_context(nc.psum_tensor("ps", [P, 8, 512], F32))

        def banks(b, n):
            return ps[:, b:b + n, :].rearrange("p a c -> p (a c)")

        def ubank(key):
            return 4 * (UNIT_AT[key] % 2)

        x_in, w_in, k_in = sem("x_in"), sem("w_in"), sem("k_in")
        wprep = sem("wprep")
        centred, squared, var_ready, sd_ready = sem("centred"), sem("squared"), sem("var_ready"), sem("sd_ready")
        norm_ready = sem("norm_ready")
        pe_unit, act_unit, dve_unit = sem("pe_unit"), sem("act_unit"), sem("dve_unit")
        split_done, dups_done, slots_set = sem("split_done"), sem("dups_done"), sem("slots_set")
        ring_filled, ring_act, ring_dve = sem("ring_filled"), sem("ring_act"), sem("ring_dve")
        ring_read = {"A": ring_act, "V": ring_dve}
        shift_ready, acts_laid = sem("shift_ready"), sem("acts_laid")
        v_staged, vs_set = sem("v_staged"), sem("vs_set")
        pv0, acc0_saved = sem("pv0"), sem("acc0_saved")
        pv1, acc1_saved = sem("pv1"), sem("acc1_saved")
        rows_set, w_staged = sem("rows_set"), sem("w_staged")
        wmax_ready, scale_ready, w_scaled = sem("wmax_ready"), sem("scale_ready"), sem("w_scaled")
        high_done = sem("high_done")
        shift1_ready = sem("shift1_ready")
        dve_step = sem("dve_step")
        pe_gate = sem("pe_gate")
        out_done = sem("out_done")

        block = ctx.enter_context(nc.Block())
        x_v = x.rearrange("(b t p) c -> p b t c", b=B, t=T)
        o_v = out.rearrange("(b t p) c -> p b t c", b=B, t=T)

        @block.sync
        def _(sp):
            for b in range(B):
                sp.dma_start(X[:, b], x_v[:, b]).then_inc(x_in, 16)
            sp.dma_start(wkqv_s[:], w_kqv).then_inc(w_in, 16)
            sp.dma_start(wo0_s[:], w_o0).then_inc(w_in, 16)
            sp.dma_start(cosT, rope_cos).then_inc(w_in, 16)
            sp.dma_start(sinT, rope_sin).then_inc(w_in, 16)
            for n, w in enumerate((w_q, w_k, w_v)):
                sp.dma_start(wqkv1[:, n, :], w).then_inc(w_in, 16)
            sp.dma_start(wo1_s[:], w_o1.rearrange("(n p) c -> p n c", p=P)).then_inc(w_in, 16)
            for b in range(B):
                sp.wait_ge(dve_unit, read_by("V", UNIT_AT[("mm", 5, b)]))
                sp.dma_start(o_v[:, b], X[:, b]).then_inc(out_done, 16)
            sp.wait_ge(out_done, 16 * B)

        W_LOADS = 8
        FREE = 2

        @block.gpsimd
        def _(pool):
            g = nc.gpsimd
            g.memset(Qs[:, :, :, 6:8, :].rearrange("p n t s c -> p (n t) (s c)"), 0.0)
            g.memset(Ks[:, :, :, 6:8, :].rearrange("p n t s c -> p (n t) (s c)"), 0.0).then_inc(slots_set, 1)
            g.memset(VS[:], 0.0).then_inc(vs_set, 1)
            pool.wait_ge(slots_set, 1)
            g.memset(Ks[:, :, :, SHIFT_SLOT, :].rearrange("p n t (h d) -> p (n t) h d", h=2)[:, :, :, 0:3],
                     1.0).then_inc(slots_set, 1)
            pool.wait_ge(vs_set, 1)
            g.memset(VS[:, :, :, :, D0:D0 + 1].rearrange("p r t h c -> p (r t h) c"), 1.0).then_inc(vs_set, 1)

            def stage_values(group, r):
                g.tensor_copy(VS[:, r, :, :, 0:D0],
                              V0[:, group].rearrange("p t (h d) -> p t h d", h=GH)).then_inc(v_staged, 1)

            pool.wait_ge(vs_set, 2)
            pool.wait_ge(act_unit, read_by("A", UNIT_AT[("qkv", B - 1, 1)]))
            stage_values(0, 0)
            stage_values(1, 1)
            with pool.Fori(1, G // 2) as i:
                for r in range(2):
                    pool.wait_ge(pv0, T * (2 * i + r - 1) + FREE)
                    stage_values(2 * i + r, r)

            pool.wait_ge(ring_filled, GROUP_LAST.filled(len(GROUP_LAST.steps) - 1, 0))
            g.memset(Q2[D1:P], 0.0)
            g.memset(K2[D1:P], 0.0).then_inc(rows_set, 1)
            pool.wait_ge(rows_set, 1)
            g.memset(K2[D1:D1 + 2], SHIFT_LOW).then_inc(rows_set, 1)
            pool.wait_ge(rows_set, 2)
            g.memset(K2[D1:D1 + 1], SHIFT_TOP).then_inc(rows_set, 1)
            pool.wait_ge(pv0, T * G + FREE)
            pool.wait_ge(rows_set, 3)
            g.memset(VA[:, :, :, :, D1:D1 + 1].rearrange("p r t h c -> p (r t h) c"), 1.0).then_inc(rows_set, 1)

            def stage_weights(pair, r):
                g.tensor_copy(ws1[:, r], wqkv1[:, 0:2, bass.ds(pair * P, P)]).then_inc(w_staged, 1)

            def weights_of(turn, k, i, pair, r):
                pool.wait_ge(ring_filled, turn.filled(k, i))
                stage_weights(pair, r)

            pool.wait_ge(w_scaled, 1)
            proj_k = {turn: [k for k, s in enumerate(turn.steps) if s[0] == "proj_k"]
                      for turns in PAIR_TURNS for turn in turns}
            for b, (first, loop, last) in enumerate(PAIR_TURNS):
                if b == 0:
                    stage_weights(0, 0)
                    stage_weights(1, 1)
                weights_of(first, proj_k[first][0], 0, 2, 0)
                weights_of(first, proj_k[first][1], 0, 3, 1)
                with pool.Fori(0, loop.times - 1) as i:
                    for r in range(2):
                        weights_of(loop, proj_k[loop][r], i, 2 * i + 4 + r, r)
                if b + 1 < B:
                    for r in range(2):
                        weights_of(loop, proj_k[loop][r], loop.times - 1, r, r)

        @block.scalar
        def _(act):
            a = nc.scalar
            for n, (dst, src) in enumerate(((raw_int, w_int), (wsc_s[:], w_scale), (bias_s[:], bias),
                                            (id_s[:], ident), (raw_masks[:, 0], mask_q),
                                            (raw_masks[:, 1], mask_k), (hm_s[:], head_mask),
                                            (raw_gu[:, 0, :], w_gate), (raw_gu[:, 1, :], w_up),
                                            (raw_d, w_down.rearrange("(n p) c -> p n c", p=P)))):
                act.dma_start(dst, src).then_inc(k_in, 16)

            def unit(key):
                act.wait_ge(pe_unit, filled(key))

            def ln_square(s, b):
                act.wait_ge(centred, B * s + b + 1)
                a.activation(W[:, b], D[:, b], ACT.Square).then_inc(squared, 1)

            def ln_root(s, b):
                act.wait_ge(var_ready, B * s + b + 1)
                a.activation(stats[:, 3, b, :], stats[:, 2, b, :], ACT.Sqrt).then_inc(sd_ready, 1)

            def turned(s, b, dst, bf=False):
                key = ("turn", s, b)
                unit(key)
                src = banks(ubank(key), 1).bitcast(BF16) if bf else banks(ubank(key), 2)
                a.activation(dst, src, ACT.Copy).then_inc(act_unit, 1)

            def norm(s):
                for b in range(B):
                    ln_square(s, b)
                for b in range(B):
                    ln_root(s, b)

            def gated(s):
                norm(s)
                for b in range(B):
                    turned(s, b, XT[:, b])
                    for c in range(HC):
                        key = ("up", s, b, c)
                        unit(key)
                        last = ("up", s, b, c - 2) if c >= 2 else ("up", s, b - 1, c + 1) if b else None
                        if last:
                            act.wait_ge(dve_unit, read_by("V", UNIT_AT[last]))
                        a.activation(ffn_g[:, c % 2 if b == 0 else (c + 1) % 2], banks(ubank(key), 2),
                                     ACT.Silu).then_inc(act_unit, 1)

            norm(0)
            for b in range(B):
                turned(0, b, XQT[:, b], True)
            norm(1)
            for b in range(B):
                turned(1, b, XT[:, b])
                for half in range(2):
                    key = ("qkv", b, half)
                    unit(key)
                    t0 = 4 * half
                    src = ps[:, ubank(key):ubank(key) + 4, 2 * P:3 * P]
                    a.activation(V0[:, b * GB:(b + 1) * GB, t0:t0 + 4, :].rearrange("p g t c -> p t g c"),
                                 src.rearrange("p t (g c) -> p t g c", g=GB), ACT.Copy).then_inc(act_unit, 1)
                    act.wait_ge(split_done, 2 * b + half + 1)
                    for stack, parts in ((Qs, Q_PARTS), (Ks, K_PARTS)):
                        for slot, part in enumerate(parts):
                            if slot != parts.index(part):
                                view = stack[:, b * NP:(b + 1) * NP, t0:t0 + 4]
                                ins = a.activation(view[:, :, :, slot, :], view[:, :, :, parts.index(part), :],
                                                   ACT.Copy)
                    ins.then_inc(dups_done, 1)

            def group_turn(turn, i, g0):
                base, par = g0
                done = 0
                for k, (kind, ahead, arg, reader) in enumerate(turn.steps):
                    if kind == "heads":
                        done += 1
                        continue
                    if reader != "A":
                        continue
                    slot = banks(turn.bank(k), 2)
                    r = (par + done + ahead) % 2
                    if kind == "k":
                        act.wait_ge(ring_filled, turn.filled(k, i))
                        src = slot.bitcast(BF16).rearrange("p (n s) -> p n s", n=2)
                        for hh in range(2):
                            ins = a.activation(KT[:, r, hh::2, :], src, ACT.Copy, scale=hm_s[:, hh:hh + 1])
                        ins.then_inc(ring_act, 1)
                    if kind == "exp":
                        t, j, n = arg
                        w = (T - t) * P
                        if j == 0:
                            act.wait_ge(pv0, T * (base + done) + t + 1)
                        act.wait_ge(ring_filled, turn.filled(k, i))
                        src = slot.rearrange("p (n c) -> p n c", n=n)[:, :, 0:w]
                        a.activation(Pr[:, t % 2, j:j + n, 0:w], src, ACT.Exp, scale=SCALE0).then_inc(ring_act, 1)
                        if t == T - 1:
                            act.wait_ge(pv0, T * (base + done + 1) + FREE)
                            a.activation(OT[:], banks(6, 2), ACT.Copy).then_inc(acc0_saved, 1)

            act.wait_ge(k_in, 16 * 10)
            group_turn(GROUP_FIRST, 0, (0, 0))
            with act.Fori(0, GROUP_LOOP.times) as i:
                group_turn(GROUP_LOOP, i, (2 * i, 0))
            group_turn(GROUP_LAST, 0, (G - 2, 0))

            act.wait_ge(ring_dve, GROUP_LAST.read("V", len(GROUP_LAST.steps) - 1, 0))
            for b in range(B):
                a.activation(D[:, b].rearrange("p t (g c) -> p t g c", g=GB),
                             acts[:, b * GB:(b + 1) * GB].rearrange("p g t c -> p t g c"), ACT.Copy).then_inc(acts_laid, 1)
            for b in range(B):
                key = ("acts", b)
                unit(key)
                a.activation(XT[:, b], banks(ubank(key), 2), ACT.Copy).then_inc(act_unit, 1)
            act.wait_ge(scale_ready, 1)
            a.activation(wqkv1[:, 0], wqkv1[:, 0], ACT.Copy, scale=qk_scale[:, 0:1])
            a.activation(wqkv1[:, 1], wqkv1[:, 1], ACT.Copy, scale=qk_scale[:, 1:2]).then_inc(w_scaled, 1)
            norm(2)
            for b in range(B):
                turned(2, b, XQT[:, b], True)
            gated(3)
            norm(4)
            for b in range(B):
                turned(4, b, XT[:, b])

            def pair_turn(turn, i, pair, first_pair, par=0):
                done = 0
                for k, (kind, h, t, reader) in enumerate(turn.steps):
                    slot = banks(turn.bank(k), 2)
                    if kind in ("proj_q", "proj_k"):
                        act.wait_ge(ring_filled, turn.filled(k, i))
                        dst, r = Q1 if kind == "proj_q" else K1, (par + done + h) % 2
                        a.activation(dst[0:D1, r, 0], slot[0:D1], ACT.Copy)
                        a.activation(dst[0:D1, r, 1], slot[D1:P], ACT.Copy).then_inc(high_done, 1)
                    if kind == "shift":
                        act.wait_ge(ring_filled, turn.filled(k, i))
                        a.activation(Q2[D1:D1 + 2, (par + done + 1) % 2, h], slot.bitcast(F16)[D1:D1 + 2, 0:S],
                                     ACT.Copy).then_inc(ring_act, 1)
                    if kind == "exp":
                        w = (T - t) * P
                        act.wait_ge(pv1, T * (2 * (first_pair + pair + done) + h) + t + 1)
                        act.wait_ge(ring_filled, turn.filled(k, i))
                        a.activation(Pr1[:, t % 2, 0:w], slot[:, 0:w], ACT.Exp,
                                     scale=exp_scale[:, 0:1]).then_inc(ring_act, 1)
                    if kind == "yT" and h == 1:
                        done += 1

            for b, (first, loop, last) in enumerate(PAIR_TURNS):
                pair_turn(first, 0, -1, b * NP, 1)
                with act.Fori(0, loop.times) as i:
                    pair_turn(loop, i, 2 * i, b * NP)
                pair_turn(last, 0, NP - 2, b * NP)
            gated(5)

        @block.vector
        def _(dve):
            v = nc.vector
            steps = [0, None, 0]

            def link(ins):
                ins.then_inc(dve_step, 1)
                steps[0] += 1
                dve.wait_ge(dve_step, steps[0] if steps[1] is None else steps[0] + steps[1] * steps[2])

            def small(ap):
                return ap.unsqueeze(2).to_broadcast([P, T, P])

            v.memset(ones_s[:], 1.0)
            v.sem_inc(pv0, FREE)
            v.sem_inc(pv1, FREE)
            dve.wait_ge(x_in, 16 * B)

            def centre(s, b):
                link(v.reduce_sum(stats[:, 0, b, :], X[:, b], AX.X))
                link(v.tensor_scalar(stats[:, 1, b, :], stats[:, 0, b, :], 1.0 / P, None, ALU.mult))
                v.tensor_tensor(D[:, b], X[:, b], small(stats[:, 1, b, :]), ALU.subtract).then_inc(centred, 1)

            def variance(s, b):
                dve.wait_ge(squared, B * s + b + 1)
                link(v.reduce_sum(stats[:, 0, b, :], W[:, b], AX.X))
                v.tensor_scalar(stats[:, 2, b, :], stats[:, 0, b, :], 1.0 / P, LN_EPS, ALU.mult,
                                ALU.add).then_inc(var_ready, 1)

            def normalise(s, b):
                dve.wait_ge(sd_ready, B * s + b + 1)
                r, t, var = stats[:, 4, b, :], stats[:, 5, b, :], stats[:, 2, b, :]
                link(v.reciprocal(r, stats[:, 3, b, :]))
                link(v.tensor_tensor(t, r, r, ALU.mult))
                link(v.tensor_tensor(t, t, var, ALU.mult))
                link(v.tensor_scalar(t, t, -0.5, 1.5, ALU.mult, ALU.add))
                link(v.tensor_tensor(r, r, t, ALU.mult))
                return v.tensor_tensor(D[:, b], D[:, b], small(r), ALU.mult)

            def norm(s, to_turn=True):
                for b in range(B):
                    centre(s, b)
                for b in range(B):
                    variance(s, b)
                for b in range(B):
                    ins = normalise(s, b)
                    if to_turn:
                        ins.then_inc(norm_ready, 1)
                    else:
                        link(ins)

            def int_ffn(s):
                norm(s, False)
                for b in range(B):
                    amax, xs, inv = stats[:, 6, b, :], stats[:, 7, b, :], stats[:, 8, b, :]
                    link(v.tensor_reduce(amax, D[:, b], AX.X, ALU.max, apply_absolute_value=True))
                    link(v.tensor_scalar(xs, amax, Q_EPS, 1.0 / 127.0, ALU.max, ALU.mult))
                    link(v.reciprocal(inv, xs))
                    link(v.tensor_tensor(W[:, b], D[:, b], small(inv), ALU.mult))
                    link(v.tensor_scalar(W[:, b], W[:, b], MAGIC, MAGIC, ALU.add, ALU.subtract))
                    v.tensor_scalar(XQ[:, b], W[:, b], 127.0, -128.0, ALU.min, ALU.max).then_inc(norm_ready, 1)
                for b in range(B):
                    key = ("mm", s, b)
                    dve.wait_ge(pe_unit, filled(key))
                    acc = banks(ubank(key), 2).rearrange("p (t c) -> p t c", t=T)
                    for t in range(T):
                        ins = v.scalar_tensor_tensor(W[:, b, t], acc[:, t], stats[:, 7, b, t:t + 1], wsc_s[:],
                                                     ALU.mult, ALU.mult)
                    ins.then_inc(dve_unit, 1)
                    dve.wait_ge(dve_unit, read_by("V", UNIT_AT[key]))
                    link(v.tensor_tensor(W[:, b], W[:, b], bias_s[:].unsqueeze(1).to_broadcast([P, T, P]), ALU.add))
                    link(v.tensor_tensor(X[:, b], X[:, b], W[:, b], ALU.add))

            def add_to_x(key, b, factor):
                dve.wait_ge(pe_unit, filled(key))
                acc = banks(ubank(key), 2).rearrange("p (t c) -> p t c", t=T)
                v.scalar_tensor_tensor(X[:, b], acc, factor, X[:, b], ALU.mult, ALU.add).then_inc(dve_unit, 1)
                dve.wait_ge(dve_unit, read_by("V", UNIT_AT[key]))

            def gated(s):
                norm(s)
                for b in range(B):
                    for c in range(HC):
                        key = ("up", s, b, c)
                        dve.wait_ge(act_unit, read_by("A", UNIT_AT[key]))
                        dve.wait_ge(pe_unit, filled(key))
                        v.tensor_tensor(ffn_h[:, c], ffn_g[:, c % 2 if b == 0 else (c + 1) % 2],
                                        banks(ubank(key) + 2, 2), ALU.mult).then_inc(dve_unit, 1)
                    add_to_x(("mm", s, b), b, 0.5)

            dve.wait_ge(k_in, 16 * 10)
            v.tensor_copy(idb_s[:], id_s[:])
            v.tensor_copy(idh_s[:], id_s[:])
            v.tensor_copy(mq_s[:], raw_masks[:, 0])
            v.tensor_copy(mk_s[:], raw_masks[:, 1])
            v.tensor_copy(wint_s[:], raw_int.bitcast(I32).rearrange("p (c two) -> p c two", two=2)[:, :, 0]).then_inc(wprep, 1)
            link(v.tensor_scalar(wsc_s[:], wsc_s[:], 0.5, None, ALU.mult))
            link(v.tensor_scalar(bias_s[:], bias_s[:], 0.5, None, ALU.mult))
            v.tensor_scalar(wg_s[:], raw_gu, W_SCALE, None, ALU.mult).then_inc(wprep, 1)
            link(v.tensor_scalar(wd_s[:], raw_d, W_SCALE, None, ALU.mult))
            int_ffn(0)

            norm(1)
            dve.wait_ge(w_in, 16 * W_LOADS)
            for b in range(B):
                for half in range(2):
                    key = ("qkv", b, half)
                    dve.wait_ge(pe_unit, filled(key))
                    dve.wait_ge(act_unit, read_by("A", UNIT_AT[key]))
                    t0 = 4 * half
                    kq = ps[:, ubank(key):ubank(key) + 4, 0:2 * P]
                    pairs = kq.rearrange("p t (n two) -> p t n two", two=2)
                    sp = sinT[:, t0:t0 + 4].rearrange("p t (n two) -> p t n two", two=2)
                    r2 = R2.rearrange("p t (n two) -> p t n two", two=2)
                    v.tensor_tensor(R, kq, cosT[:, t0:t0 + 4], ALU.mult)
                    v.tensor_tensor(r2[:, :, :, 0], pairs[:, :, :, 1], sp[:, :, :, 0], ALU.mult)
                    v.tensor_tensor(r2[:, :, :, 1], pairs[:, :, :, 0], sp[:, :, :, 1], ALU.mult).then_inc(dve_unit, 1)
                    dve.wait_ge(dve_unit, read_by("V", UNIT_AT[key]))
                    link(v.tensor_tensor(R, R, R2, ALU.add))
                    for n, (stack, parts) in enumerate(((Ks, K_PARTS), (Qs, Q_PARTS))):
                        rest = R[:, :, n * P:(n + 1) * P].rearrange("p t (n c) -> p t n c", n=NP)
                        view = stack[:, b * NP:(b + 1) * NP, t0:t0 + 4]
                        for part in range(3):
                            dst = view[:, :, :, parts.index(part), :].rearrange("p n t c -> p t n c")
                            ins = v.tensor_copy(dst, rest)
                            if part < 2:
                                link(ins)
                                link(v.tensor_tensor(rest, rest, dst, ALU.subtract))
                    ins.then_inc(split_done, 1)

            v.tensor_reduce(wmax[:, 0:1], wqkv1[:, 0], AX.X, ALU.max, apply_absolute_value=True)
            v.tensor_reduce(wmax[:, 1:2], wqkv1[:, 1], AX.X, ALU.max,
                            apply_absolute_value=True).then_inc(wmax_ready, 1)

            def group_turn(turn, i, base, next_group):
                done = 0
                for k, (kind, ahead, arg, reader) in enumerate(turn.steps):
                    if reader != "V":
                        continue
                    dve.wait_ge(ring_filled, turn.filled(k, i))
                    slot = banks(turn.bank(k), 2)
                    if kind == "max":
                        t, j, n = arg
                        src = slot.rearrange("p (n c) -> p n c", n=n)[:, :, 0:(t + 1) * P]
                        v.tensor_reduce(mx0[:, t, j:j + n], src, AX.X, ALU.max, negate=True).then_inc(ring_dve, 1)
                        if (t, j + n) == (T - 1, GH):
                            dve.wait_ge(ring_dve, turn.read("V", k, i))
                            view = Qs[:, bass.ds(2 * (next_group + done), 2), :, SHIFT_SLOT, :]
                            view = view.rearrange("p a t (h d) -> p a t h d", h=2)
                            by_pair = [m.rearrange("p t (a h) -> p a t h", a=2) for m in (mx0[:], mr0[:, 0], mr0[:, 1])]
                            link(v.tensor_copy(view[:, :, :, :, 0], by_pair[0]))
                            link(v.tensor_tensor(by_pair[1], by_pair[0], view[:, :, :, :, 0], ALU.subtract))
                            link(v.tensor_copy(view[:, :, :, :, 1], by_pair[1]))
                            link(v.tensor_tensor(by_pair[2], by_pair[1], view[:, :, :, :, 1], ALU.subtract))
                            v.tensor_copy(view[:, :, :, :, 2], by_pair[2]).then_inc(shift_ready, 1)
                    if kind in ("q", "shifted_q"):
                        dst = QT if kind == "q" else QmT
                        v.tensor_copy(dst[:], slot.bitcast(BF16).rearrange("p (n s) -> p n s", n=2)).then_inc(ring_dve, 1)
                    if kind == "heads":
                        src = slot.rearrange("p (t h c) -> p t h c", t=T, h=GH)
                        link(v.reciprocal(rs0[:], src[:, :, :, D0]))
                        v.tensor_tensor(acts[:, base + done].rearrange("p t (h d) -> p t h d", h=GH),
                                        src[:, :, :, 0:D0], rs0[:].unsqueeze(3).to_broadcast([P, T, GH, D0]),
                                        ALU.mult).then_inc(ring_dve, 1)
                        done += 1

            def looped(times, links, body):
                start = steps[0]
                with dve.Fori(0, times) as i:
                    steps[1:] = [i, links]
                    body(i)
                assert steps[0] == start + links, (steps[0] - start, links)
                steps[:] = [start + links * times, None, 0]

            group_turn(GROUP_FIRST, 0, 0, 0)
            looped(GROUP_LOOP.times, 10, lambda i: group_turn(GROUP_LOOP, i, 2 * i, 2 * i + 1))
            group_turn(GROUP_LAST, 0, G - 2, G - 1)
            for b in range(B):
                add_to_x(("mm", 1, b), b, 1.0)
            dve.wait_ge(pe_unit, filled(("wscale",)))
            v.tensor_scalar(wsum[:], ps[:, ubank(("wscale",)), 0:2], 1e-15, None, ALU.max).then_inc(dve_unit, 1)
            dve.wait_ge(dve_unit, read_by("V", UNIT_AT[("wscale",)]))
            link(v.reciprocal(wsum[:], wsum[:]))
            link(v.tensor_scalar(wsum[:], wsum[:], QK_BOUND / float(P) ** 0.5, None, ALU.mult))
            link(v.tensor_scalar(qk_scale[:].bitcast(I32), wsum[:].bitcast(I32), 0x7F800000, None,
                                 ALU.bitwise_and))
            link(v.tensor_tensor(exp_scale[:], qk_scale[:, 0:1], qk_scale[:, 1:2], ALU.mult))
            link(v.reciprocal(exp_scale[:], exp_scale[:]))
            link(v.tensor_scalar(exp_scale[:], exp_scale[:], SCALE1, None, ALU.mult))
            v.sem_inc(scale_ready, 1)
            int_ffn(2)
            gated(3)
            norm(4)

            def pair_turn(turn, i, pair, first_pair, par=0):
                done = 0

                owed = False

                def weighted(h):
                    n = 2 * (first_pair + pair + done) + h
                    dve.wait_ge(pv1, T * (n + 1) + FREE)
                    acc = ps[:, 6:8, 0:4 * VW].rearrange("p a (t c) -> p a t c", t=4)
                    rs = rs1[:, h].rearrange("p (a t) -> p a t", a=2)
                    link(v.reciprocal(rs, acc[:, :, :, D1]))
                    v.tensor_tensor(Y1[:, :, h * D1:(h + 1) * D1].rearrange("p (a t) c -> p a t c", a=2),
                                    acc[:, :, :, 0:D1], rs.unsqueeze(3).to_broadcast([P, 2, 4, D1]),
                                    ALU.mult).then_inc(acc1_saved, 1)

                for k, (kind, h, t, reader) in enumerate(turn.steps):
                    if kind == "exp" and (h, t) == (1, 1):
                        weighted(0)
                    if kind == "exp":
                        owed = h == 1
                    if owed and (kind == "proj_k" or kind == "yT"):
                        weighted(1)
                        owed = False
                    if reader == "V":
                        dve.wait_ge(ring_filled, turn.filled(k, i))
                        slot = banks(turn.bank(k), 2)
                        r = (par + done + h) % 2
                        if kind == "max":
                            v.tensor_reduce(mx1[:, h, t:t + 1], slot[:, 0:(t + 1) * P], AX.X, ALU.max,
                                            negate=True).then_inc(ring_dve, 1)
                            if t == T - 1:
                                dve.wait_ge(ring_dve, turn.read("V", k, i))
                                link(v.tensor_scalar(mx1[:, h], mx1[:, h], 1 / SHIFT_TOP, None, ALU.mult))
                                link(v.tensor_copy(sh1[:, h, :, 0], mx1[:, h]))
                                link(v.tensor_tensor(mx1[:, h], mx1[:, h], sh1[:, h, :, 0], ALU.subtract))
                                v.tensor_scalar(sh1[:, h, :, 1], mx1[:, h], SHIFT_TOP / SHIFT_LOW, None,
                                                ALU.mult).then_inc(shift1_ready, 1)
                        if kind in ("proj_q", "proj_k"):
                            n = 2 * (first_pair + pair + done + h) + (2 if kind == "proj_k" else 1)
                            dve.wait_ge(high_done, n)
                            high = Q1 if kind == "proj_q" else K1
                            for head in range(2):
                                low = Q2[0:D1, r, head] if kind == "proj_q" else K1[D1:P, r, head]
                                v.tensor_tensor(low, slot[head * D1:(head + 1) * D1], high[0:D1, r, head],
                                                ALU.subtract)
                            copy = Q1[D1:P, r] if kind == "proj_q" else K2[0:D1, r]
                            v.tensor_copy(copy, high[0:D1, r]).then_inc(ring_dve, 1)
                        if kind == "proj_v":
                            v.tensor_copy(VA[:, r, :, :, 0:D1],
                                          slot.rearrange("p (t h c) -> p t h c", t=T, h=2)).then_inc(ring_dve, 1)
                        if kind == "yT":
                            v.tensor_copy(YT[:, bass.ds(pair + done, 1), 512 * h:512 * h + 512].rearrange(
                                "p n s -> p (n s)"), slot[:, 0:512]).then_inc(ring_dve, 1)
                    if kind == "yT" and h == 1:
                        done += 1

            for b, (first, loop, last) in enumerate(PAIR_TURNS):
                if b == 0:
                    dve.wait_ge(rows_set, 4)
                pair_turn(first, 0, -1, b * NP, 1)
                looped(loop.times, 16, lambda i: pair_turn(loop, i, 2 * i, b * NP))
                pair_turn(last, 0, NP - 2, b * NP)
                add_to_x(("mm", 4, b), b, 1.0)
            gated(5)

        @block.tensor
        def _(pe):
            te = nc.tensor

            def unit(key, ring=None):
                n = UNIT_AT[key]
                if n >= 2:
                    for e, s in (("A", act_unit), ("V", dve_unit)):
                        if e in UNITS[n - 2][1]:
                            pe.wait_ge(s, read_by(e, n - 2))
                if ring:
                    for e in "AV":
                        pe.wait_ge(ring_read[e], ring.read(e, len(ring.steps) - 1, 0))
                return ubank(key)

            def turn_half(key, src, ident_ap, bf=False, ring=None):
                b0 = unit(key, ring)
                for t in range(T):
                    if bf:
                        dst = banks(b0, 1).bitcast(BF16)[:, t * P:(t + 1) * P]
                    else:
                        dst = banks(b0, 2)[:, t * P:(t + 1) * P]
                    ins = te.transpose(dst, src(t), ident_ap)
                ins.then_inc(pe_unit, 1)

            def int_ffn(s):
                for b in range(B):
                    pe.wait_ge(norm_ready, B * s + b + 1)
                    turn_half(("turn", s, b), lambda t: XQ[:, b, t], idb_s[:], True)
                    key = ("mm", s, b)
                    b0 = unit(key)
                    pe.wait_ge(act_unit, read_by("A", UNIT_AT[("turn", s, b)]))
                    for t in range(T):
                        ins = te.matmul(banks(b0, 2)[:, t * P:(t + 1) * P], XQT[:, b, t * P:(t + 1) * P],
                                        wint_s[:], start=True, stop=True)
                    ins.then_inc(pe_unit, 1)

            def gated(s):
                for b in range(B):
                    pe.wait_ge(norm_ready, B * s + b + 1)
                    turn_half(("turn", s, b), lambda t: D[:, b, t], id_s[:])
                    for c in range(HC):
                        key = ("up", s, b, c)
                        b0 = unit(key)
                        pe.wait_ge(act_unit, read_by("A", UNIT_AT[("turn", s, b)]))
                        for m in range(2):
                            for n in range(2):
                                ins = te.matmul(ps[:, b0 + 2 * m + n], wg_s[:, m, c * P:(c + 1) * P],
                                                XT[:, b, 512 * n:512 * n + 512], start=True, stop=True)
                        ins.then_inc(pe_unit, 1)
                    key = ("mm", s, b)
                    b0 = unit(key)
                    pe.wait_ge(dve_unit, read_by("V", UNIT_AT[("up", s, b, HC - 1)]))
                    for t in range(T):
                        for c in range(HC):
                            ins = te.matmul(banks(b0, 2)[:, t * P:(t + 1) * P], ffn_h[:, c, t * P:(t + 1) * P],
                                            wd_s[:, c], start=c == 0, stop=c == HC - 1)
                    ins.then_inc(pe_unit, 1)

            pe.wait_ge(k_in, 16 * 10)
            pe.wait_ge(wprep, 2)
            int_ffn(0)
            pe.wait_ge(w_in, 16 * W_LOADS)
            for b in range(B):
                pe.wait_ge(norm_ready, B * 1 + b + 1)
                turn_half(("turn", 1, b), lambda t: D[:, b, t], id_s[:])
                for half in range(2):
                    key = ("qkv", b, half)
                    b0 = unit(key)
                    pe.wait_ge(act_unit, read_by("A", UNIT_AT[("turn", 1, b)]))
                    for q in range(4):
                        t = 4 * half + q
                        ins = te.matmul(ps[:, b0 + q, 0:3 * P], XT[:, b, t * P:(t + 1) * P], wkqv_s[:],
                                        start=True, stop=True)
                    ins.then_inc(pe_unit, 1)

            def free_slot(turn, k, i):
                f = turn.freed(k, i)
                if f:
                    pe.wait_ge(ring_read[f[0]], f[1])
                return banks(turn.bank(k), 2)

            def scores(slot, off, lhsT, rhs, w, mask, mask_at):
                for c in range(0, w, 512):
                    n = min(512, w - c)
                    diag = c <= mask_at < c + n
                    ins = te.matmul(slot[:, off + c:off + c + n], lhsT, rhs[:, c:c + n], start=True, stop=not diag)
                    if diag:
                        ins = te.matmul(slot[:, off + mask_at:off + mask_at + P], idb_s[:], mask[:],
                                        start=False, stop=True)
                return ins

            def group_turn(turn, i, base, par):
                done = 0
                waiting = None

                def weigh(t, read):
                    gcount = base + done
                    pe.wait_ge(ring_act, read)
                    if t == 0:
                        pe.wait_ge(acc0_saved, gcount)
                        pe.wait_ge(v_staged, gcount + 1)
                    q0 = t * P
                    for bank in range(2):
                        a0, a1 = max(q0, 512 * bank), 512 * (bank + 1)
                        if a0 >= a1:
                            continue
                        for j in range(GH):
                            ins = te.matmul(ps[32 * j:32 * j + 32, 6 + bank, a0 - 512 * bank:512],
                                            VS[:, (par + done) % 2, t, j], Pr[:, t % 2, j, a0 - q0:a1 - q0],
                                            start=t == 0, stop=t == 4 * bank + 3, tile_position=(0, 32 * j))
                    ins.then_inc(pv0, 1)

                for k, (kind, ahead, arg, reader) in enumerate(turn.steps):
                    g = base + done + ahead
                    r = (par + done + ahead) % 2
                    if kind == "exp" and arg[:2] == (0, 0):
                        last = [q for q in range(k) if turn.steps[q][0] == "shifted_q"]
                        if last:
                            pe.wait_ge(ring_dve, turn.read("V", last[-1], i))
                        else:
                            pe.wait_ge(ring_dve, turn.c0["V"] + i * turn.reads("V"))
                    if kind == "max" and arg[:2] == (0, 0):
                        last = [q for q in range(k) if turn.steps[q][0] == "q"]
                        for e in "AV":
                            if last:
                                pe.wait_ge(ring_read[e], turn.read(e, last[-1], i))
                            else:
                                pe.wait_ge(ring_read[e], turn.c0[e] + i * turn.reads(e))
                    if kind == "heads":
                        pe.wait_ge(acc0_saved, base + done + 1)
                    if kind == "shifted_q":
                        pe.wait_ge(shift_ready, g + 1)
                    slot = free_slot(turn, k, i)
                    if kind == "max":
                        t, j, n = arg
                        for q in range(n):
                            ins = scores(slot, q * (1024 // n), QT[:, (j + q) // 2, t * P:(t + 1) * P],
                                         KT[:, r, j + q], (t + 1) * P, mq_s, t * P)
                    if kind == "exp":
                        t, j, n = arg
                        for q in range(n):
                            ins = scores(slot, q * (1024 // n), KT[:, r, j + q, t * P:(t + 1) * P],
                                         QmT[:, (j + q) // 2, t * P:], (T - t) * P, mk_s, 0)
                    if kind in ("k", "q", "shifted_q"):
                        te.sem_inc(pe_gate, 1)
                        src = Ks if kind == "k" else Qs
                        dst = slot.bitcast(BF16)
                        for pair in range(2):
                            for t in range(T):
                                c = pair * S + t * P
                                rows = src[:, bass.ds(2 * g + pair, 1), t].rearrange("p n s c -> p (n s c)")
                                ins = te.transpose(dst[:, c:c + P], rows, idb_s[:])
                    if kind == "heads":
                        for t in range(T):
                            ins = te.transpose(slot[:, t * P:(t + 1) * P], OT[:, t * P:(t + 1) * P], id_s[:])
                    ins.then_inc(ring_filled, 1)
                    nxt = turn.steps[k + 1][0] if k + 1 < len(turn.steps) else None
                    if waiting and (kind == "exp" or nxt == "heads"):
                        weigh(*waiting)
                        waiting = None
                    if kind == "exp" and arg[1] + arg[2] == GH:
                        waiting = (arg[0], turn.read("A", k, i))
                        if nxt == "heads":
                            weigh(*waiting)
                            waiting = None
                    if kind == "heads":
                        done += 1

            for n in range(2):
                u = UNIT_AT[("qkv", B - 1, 1)] - n
                pe.wait_ge(act_unit, read_by("A", u))
                pe.wait_ge(dve_unit, read_by("V", u))
            pe.wait_ge(dups_done, 2 * B)
            pe.wait_ge(slots_set, 2)
            group_turn(GROUP_FIRST, 0, 0, 0)
            with pe.Fori(0, GROUP_LOOP.times) as i:
                group_turn(GROUP_LOOP, i, 2 * i, 0)
            group_turn(GROUP_LAST, 0, G - 2, 0)

            for b in range(B):
                pe.wait_ge(acts_laid, b + 1)
                turn_half(("acts", b), lambda t: D[:, b, t], id_s[:], ring=GROUP_LAST)
                key = ("mm", 1, b)
                b0 = unit(key)
                pe.wait_ge(act_unit, read_by("A", UNIT_AT[("acts", b)]))
                for t in range(T):
                    ins = te.matmul(banks(b0, 2)[:, t * P:(t + 1) * P], XT[:, b, t * P:(t + 1) * P], wo0_s[:],
                                    start=True, stop=True)
                ins.then_inc(pe_unit, 1)
            b0 = unit(("wscale",))
            pe.wait_ge(wmax_ready, 1)
            te.matmul(ps[:, b0, 0:2], ones_s[:], wmax[:], start=True, stop=True).then_inc(pe_unit, 1)
            int_ffn(2)
            gated(3)
            for b in range(B):
                pe.wait_ge(norm_ready, B * 4 + b + 1)
                turn_half(("turn", 4, b), lambda t: D[:, b, t], id_s[:])

            def pair_turn(turn, i, pair, first_pair, b, par=0):
                done = 0
                waiting = None

                def weigh(h, t, read, r, n):
                    pe.wait_ge(ring_act, read)
                    if t == 0:
                        pe.wait_ge(acc1_saved, n)
                    for q in range(t, T):
                        c = (q % 4) * VW
                        ins = te.matmul(ps[:, 6 + q // 4, c:c + D1 + 1], Pr1[:, t % 2, (q - t) * P:(q - t + 1) * P],
                                        VA[:, r, t, h, 0:D1 + 1], start=t == 0 and q % 4 == 0, stop=t == q,
                                        skip_group_check=True)
                    ins.then_inc(pv1, 1)

                def read_before(e, k, kinds):
                    last = [q for q in range(k) if turn.steps[q][0] in kinds]
                    if last:
                        pe.wait_ge(ring_read[e], turn.read(e, last[-1], i))
                    else:
                        pe.wait_ge(ring_read[e], turn.c0[e] + i * turn.reads(e))

                def products(kind, r, h, t, slot):
                    c0, w = (0, (t + 1) * P) if kind == "max" else (t * P, (T - t) * P)
                    at = t * P if kind == "max" else 0
                    for c in range(0, w, 512):
                        n = min(512, w - c)
                        diag = c <= at < c + n
                        tile, cols = slice(t * P, (t + 1) * P), slice(c0 + c, c0 + c + n)
                        if kind == "max":
                            ins = te.matmul(slot[:, c:c + n], Q1[:, r, h, tile], K1[:, r, h, cols],
                                            start=True, stop=not diag)
                        else:
                            te.matmul(slot[:, c:c + n], K1[:, r, h, tile], Q1[:, r, h, cols],
                                      start=True, stop=False)
                            ins = te.matmul(slot[:, c:c + n], K2[:, r, h, tile], Q2[:, r, h, cols],
                                            start=False, stop=not diag)
                        if diag:
                            ins = te.matmul(slot[:, at:at + P], idb_s[:], (mq_s if kind == "max" else mk_s)[:],
                                            start=False, stop=True)
                    return ins

                for k, (kind, h, t, reader) in enumerate(turn.steps):
                    here = (par + done) % 2
                    whole = first_pair + pair + done
                    if kind == "max" and (h, t) == (0, 0):
                        read_before("V", k, ("proj_v",))
                    if kind == "shift":
                        pe.wait_ge(shift1_ready, 2 * (whole + 1) + h + 1)
                    if kind == "exp" and t == 0:
                        read_before("A", k, ("shift",))
                    if kind == "proj_q":
                        pe.wait_ge(w_staged, whole + h + 1)
                    if kind == "yT" and h == 0:
                        pe.wait_ge(acc1_saved, 2 * whole + 2)
                    slot = free_slot(turn, k, i)
                    if kind == "max":
                        ins = products(kind, (here + 1) % 2, h, t, slot)
                    if kind == "exp":
                        ins = products(kind, here, h, t, slot)
                    if kind == "shift":
                        te.sem_inc(pe_gate, 1)
                        for q in range(T):
                            ins = te.transpose(slot.bitcast(F16)[D1:D1 + 2, q * P:(q + 1) * P], sh1[:, h, q],
                                               idh_s[:])
                    if kind in ("proj_q", "proj_k"):
                        for n in range(2):
                            ins = te.matmul(slot[:, 512 * n:512 * n + 512], ws1[:, (here + h) % 2, int(kind == "proj_k")],
                                            XT[:, b, 512 * n:512 * n + 512], start=True, stop=True)
                    if kind == "proj_v":
                        for q in range(T):
                            ins = te.matmul(slot[:, q * P:(q + 1) * P], XT[:, b, q * P:(q + 1) * P],
                                            wqkv1[:, 2, bass.ds((pair + done + h) * P, P)], start=True, stop=True)
                    if kind == "yT":
                        for q in range(4):
                            ins = te.transpose(slot[:, q * P:(q + 1) * P], Y1[:, 4 * h + q], id_s[:])
                    ins.then_inc(ring_filled, 1)
                    after = turn.steps[k + 1][:2] if k + 1 < len(turn.steps) else None
                    if waiting and (kind in ("exp", "proj_q") or after in (("shift", 1), ("yT", 0))):
                        weigh(*waiting)
                        waiting = None
                    if kind == "exp":
                        waiting = (h, t, turn.read("A", k, i), here, 2 * whole + h)
                        if after == ("yT", 0):
                            weigh(*waiting)
                            waiting = None
                    if kind == "yT" and h == 1:
                        done += 1

            for b, (first, loop, last) in enumerate(PAIR_TURNS):
                if b == 0:
                    for n in range(2):
                        u = UNIT_AT[("turn", 4, B - 1)] - n
                        pe.wait_ge(act_unit, read_by("A", u))
                    pe.wait_ge(rows_set, 4)
                else:
                    pe.wait_ge(dve_unit, read_by("V", UNIT_AT[("mm", 4, b - 1)]))
                pair_turn(first, 0, -1, b * NP, b, 1)
                with pe.Fori(0, loop.times) as i:
                    pair_turn(loop, i, 2 * i, b * NP, b)
                pair_turn(last, 0, NP - 2, b * NP, b)
                key = ("mm", 4, b)
                b0 = unit(key, last)
                for t in range(T):
                    for n in range(NP):
                        ins = te.matmul(banks(b0, 2)[:, t * P:(t + 1) * P], YT[:, n, t * P:(t + 1) * P],
                                        wo1_s[:, n], start=n == 0, stop=n == NP - 1)
                ins.then_inc(pe_unit, 1)
            gated(5)


def _constants():
    import numpy as np

    eye = np.eye(P, dtype=np.float32)
    row, col = np.arange(P)[:, None], np.arange(P)[None, :]
    inv_freq = np.float32(1.0) / np.float32(10000.0) ** (np.arange(0, D0, 2, dtype=np.float32) / np.float32(D0))
    ang = np.arange(S, dtype=np.float32)[:, None] * inv_freq[None, :]
    cos = np.tile(np.repeat(np.cos(ang), 2, axis=1), (1, 2 * H))
    sin = np.repeat(np.sin(ang), 2, axis=1)
    sin[:, 0::2] *= -1
    sin = np.tile(sin, (1, 2 * H))
    by_tile = lambda a: np.ascontiguousarray(a.reshape(T, P, -1).transpose(1, 0, 2)).astype(np.float32)
    hh = (np.arange(P) // D0) % 2
    return {
        "ident": eye,
        "mask_q": np.where(col > row, np.float32(-1e30), np.float32(0)),
        "mask_k": np.where(col < row, np.float32(-1e30), np.float32(0)),
        "head_mask": np.stack([hh == 0, hh == 1], axis=1).astype(np.float32),
        "rope_cos": by_tile(cos),
        "rope_sin": by_tile(sin),
    }


def kernel(L0_attn_X, L0_attn_W_KQV, L0_attn_W_O, L0_ffn_weight_q, L0_ffn_weight_scale, L0_ffn_bias,
           L1_attn_w_q, L1_attn_w_k, L1_attn_w_v, L1_attn_w_o, L1_ffn_w_gate, L1_ffn_w_up, L1_ffn_w_down):
    import numpy as np
    import concourse.bacc as bacc
    from concourse.bass_utils import run_bass_kernel_spmd

    def lay(a):
        return np.ascontiguousarray(a)

    arrays = {
        "x": lay(L0_attn_X).reshape(B * S, P),
        "w_kqv": lay(np.asarray(L0_attn_W_KQV).T),
        "w_o0": lay(np.asarray(L0_attn_W_O).T),
        "w_int": lay(np.asarray(L0_ffn_weight_q).T).astype(np.int64),
        "w_scale": lay(np.broadcast_to(np.asarray(L0_ffn_weight_scale), (P, P))),
        "bias": lay(np.broadcast_to(np.asarray(L0_ffn_bias), (P, P))),
        "w_q": lay(np.asarray(L1_attn_w_q).reshape(H * D1, P).T),
        "w_k": lay(np.asarray(L1_attn_w_k).reshape(H * D1, P).T),
        "w_v": lay(np.asarray(L1_attn_w_v).reshape(H * D1, P).T),
        "w_o1": lay(L1_attn_w_o),
        "w_gate": lay(np.asarray(L1_ffn_w_gate).T),
        "w_up": lay(np.asarray(L1_ffn_w_up).T),
        "w_down": lay(np.asarray(L1_ffn_w_down).T),
    }
    arrays.update(_constants())
    nc = bacc.Bacc("TRN2", target_bir_lowering=False, num_devices=1)
    args = [nc.dram_tensor(f"in_{n}_dram", a.shape, mybir.dt.from_np(a.dtype), kind="ExternalInput").ap()
            for n, a in arrays.items()]
    args.append(nc.dram_tensor("out_0_dram", (B * S, P), F32, kind="ExternalOutput").ap())
    macaron_block_kernel(nc, *args)
    r = run_bass_kernel_spmd(nc, [{f"in_{n}_dram": a for n, a in arrays.items()}], core_ids=[0])
    return r.results[0]["out_0_dram"].reshape(B, S, P)
```

```python
from contextlib import ExitStack

import concourse.bass as bass
from concourse import mybir

ALU = mybir.AluOpType
ACT = mybir.ActivationFunctionType
AX = mybir.AxisListType
F32 = mybir.dt.float32
BF16 = mybir.dt.bfloat16
F16 = mybir.dt.float16
I32 = mybir.dt.int32
I64 = mybir.dt.int64

P = 128
B = 2
S = 1024
T = S // P
H = 16
D0 = P // H
D1 = 64
HID = 384
HC = HID // P
SLOTS = 8
GH = 4
G = B * H // GH
GB = H // GH
SHIFT_TOP, SHIFT_LOW = 2.0**14, 2.0**3
QK_BOUND = 4096.0
VW = 66
NP = H // 2
LN_EPS = 1e-5
Q_EPS = 1e-6
MAGIC = 1.5 * 2.0**23
SCALE0 = float(D0) ** -0.5
SCALE1 = float(D1) ** -0.5
W_SCALE = 1.0 / 127.0
RING = 3

Q_PARTS = (0, 0, 1, 1, 0, 2)
K_PARTS = (0, 1, 0, 1, 2, 0)
SHIFT_SLOT = 6


def plan_units():
    units = []

    def int_ffn(s):
        for b in range(B):
            units.append((("turn", s, b), "A"))
            units.append((("mm", s, b), "V"))

    def gated_ffn(s):
        for b in range(B):
            units.append((("turn", s, b), "A"))
            for c in range(HC):
                units.append((("up", s, b, c), "AV"))
            units.append((("mm", s, b), "V"))

    int_ffn(0)
    for b in range(B):
        units.append((("turn", 1, b), "A"))
        for half in range(2):
            units.append((("qkv", b, half), "AV"))
    for b in range(B):
        units.append((("acts", b), "A"))
        units.append((("mm", 1, b), "V"))
    units.append((("wscale",), "V"))
    int_ffn(2)
    gated_ffn(3)
    for b in range(B):
        units.append((("turn", 4, b), "A"))
    gated_ffn(5)
    return units


UNITS = plan_units()
UNIT_AT = {key: n for n, (key, _) in enumerate(UNITS)}


def filled(key):
    return UNIT_AT[key] + 1


def read_by(engine, n):
    return sum(engine in who for _, who in UNITS[: n + 1])


def grouped(widths):
    steps = []
    for t, w in widths:
        n = 1 if w > 512 else 2 if w > 256 else 4
        steps += [(t, j, n) for j in range(0, GH, n)]
    return steps


MAX_STEPS = grouped([(t, (t + 1) * P) for t in range(T)])
EXP_STEPS = grouped([(t, (T - t) * P) for t in range(T)])


def group_steps(exps, maxes, turn_next, turn_after):
    steps = []
    for n in range(len(EXP_STEPS)):
        if exps:
            steps.append(("exp", 0, EXP_STEPS[n], "A"))
        if maxes:
            steps.append(("max", 1, MAX_STEPS[n], "V"))
    if turn_next:
        steps.append(("shifted_q", 1, None, "V"))
    if exps:
        steps.append(("heads", 0, None, "V"))
    if turn_after:
        steps.append(("k", 1, None, "A"))
        steps.append(("q", 1, None, "V"))
    return steps


Q_AT, K_AT, SHIFT_AT = (0, 2), (1, 2), (3, 3)
MAX_AT = ((0,), (1, 2), (3,), (4,), (5,), (6,), (7,), ())


def pair_steps(exps, maxes, project):
    steps = []
    for h in range(2):
        for t in range(T):
            if exps:
                steps.append(("exp", h, t, "A"))
            if maxes:
                steps += [("max", h, m, "V") for m in MAX_AT[t]]
            if t == SHIFT_AT[h] and (exps if h == 0 else maxes):
                steps.append(("shift", 1 - h, None, "A"))
            if project and (h, t) == Q_AT:
                steps.append(("proj_q", 2, None, "A"))
            if project and (h, t) == K_AT:
                steps.append(("proj_k", 2, None, "A"))
    if project:
        steps.append(("proj_v", 2, None, "A"))
    if exps:
        steps += [("yT", 0, None, "A"), ("yT", 1, None, "A")]
    return steps


class Turn:

    def __init__(self, steps, times=1, after=None):
        self.steps, self.times = steps, times
        self.before = after
        self.n0 = after.n0 + after.times * len(after.steps) if after else 0
        self.c0 = {e: (after.c0[e] + after.times * after.reads(e)) if after else 0 for e in "AV"}
        assert times == 1 or len(steps) % RING == 0

    def reads(self, e, upto=None):
        return sum(s[-1] == e for s in self.steps[:upto])

    def filled(self, k, i):
        return self.n0 + k + 1 + i * len(self.steps)

    def read(self, e, k, i):
        return self.c0[e] + self.reads(e, k + 1) + i * self.reads(e)

    def bank(self, k):
        return 2 * ((self.n0 + k) % RING)

    def freed(self, k, i):
        if k >= RING:
            e = self.steps[k - RING][-1]
            return [(e, self.read(e, k - RING, i))]
        back = RING - k
        last = self.before
        if last is None:
            return []
        if self.times > 1 and [s[-1] for s in self.steps[-RING:]] != [s[-1] for s in last.steps[-RING:]]:
            return [(e, self.c0[e] + i * self.reads(e)) for e in "AV"] if k == 0 else []
        e = last.steps[-back][-1]
        later = sum(s[-1] == e for s in last.steps[len(last.steps) - back + 1 :])
        return [(e, self.c0[e] - later + i * self.reads(e))]


GROUP_FIRST = Turn(
    [("k", 0, None, "A"), ("q", 0, None, "V")]
    + [("max", 0, m, "V") for m in MAX_STEPS]
    + [("shifted_q", 0, None, "V"), ("k", 1, None, "A"), ("q", 1, None, "V")]
)
GROUP_LOOP = Turn(2 * group_steps(True, True, True, True), (G - 2) // 2, GROUP_FIRST)
GROUP_LAST = Turn(
    group_steps(True, True, True, False) + group_steps(True, False, False, False), 1, GROUP_LOOP
)
QK_SETS = 3
PAIR_FIRST = Turn(
    [("proj_q", 1, None, "A"), ("proj_k", 1, None, "A"), ("proj_q", 2, None, "A"), ("proj_k", 2, None, "A")]
    + pair_steps(False, True, False) + [("proj_v", 1, None, "A"), ("proj_v", 2, None, "A")], 1, GROUP_LAST
)


def pair_turns():
    turns, after = [], PAIR_FIRST
    for b in range(B):
        loop = Turn(QK_SETS * pair_steps(True, True, True), (NP - 2) // QK_SETS, after)
        ends = b == B - 1
        last = Turn(pair_steps(True, True, not ends) + pair_steps(True, not ends, not ends)
                    + [("wo", 0, None, "V")], 1, loop)
        turns.append((loop, last))
        after = last
    return turns


PAIR_TURNS = pair_turns()


def macaron_block_kernel(nc, x, w_kqv, w_o0, w_int, w_scale, bias, w_q, w_k, w_v, w_o1, w_gate, w_up,
                         w_down, ident, mask_q, mask_k, head_mask, rope_cos, rope_sin, out):
    ctx = ExitStack()
    with ctx:
        def sb(name, shape, dt=F32):
            return ctx.enter_context(nc.sbuf_tensor(name, shape, dt))

        def sem(name):
            return ctx.enter_context(nc.semaphore(name))

        X = sb("X", [P, B, T, P])
        work = sb("work", [P, 2, B, T, P])
        D = work[:, 0]
        W = work[:, 1]
        XQ = sb("XQ", [P, B, T, P], BF16)
        XQT = sb("XQT", [P, B, S], BF16)
        XT = sb("XT", [P, B, S])
        ffn_h = sb("ffn_h", [P, HC, S])
        big = sb("big", [P, 16384])
        Pr = sb("Pr", [P, 2, GH, S])
        ffn_g = Pr[:, 0, 2:4, :]
        V0 = sb("V0", [P, G, T, GH * D0])
        VS = sb("VS", [P, 2, T, GH, 32])
        OT = sb("OT", [P, S])
        acts = sb("acts", [P, G, T, GH * D0])
        stats = sb("stats", [P, 16, B, T])
        mx0 = sb("mx0", [P, T, GH])
        mr0 = sb("mr0", [P, 2, T, GH])
        rs0 = sb("rs0", [P, T, GH])
        mx1 = sb("mx1", [P, 2, T])
        sh1 = sb("sh1", [P, 2, T, 2], F16)
        rs1 = sb("rs1", [P, 2, T])
        wmax = sb("wmax", [P, 2])
        wsum = sb("wsum", [P, 2])
        qk_scale = sb("qk_scale", [P, 2])
        exp_scale = sb("exp_scale", [P, 1])
        wkqv_s = sb("wkqv_s", [P, 3 * P])
        wo0_s = sb("wo0_s", [P, P])
        wint_s = sb("wint_s", [P, P], BF16)
        wsc_s = sb("wsc_s", [P, P])
        bias_s = sb("bias_s", [P, P])
        wqkv1 = sb("wqkv1", [P, 3, H * D1])
        wo1_s = sb("wo1_s", [P, NP, P])
        wg_s = sb("wg_s", [P, 2, HID])
        wd_s = sb("wd_s", [P, HC, P])
        id_s = sb("id_s", [P, P])
        idb_s = sb("idb_s", [P, P], BF16)
        idh_s = sb("idh_s", [P, P], F16)
        ones_s = sb("ones_s", [P, P])
        mq_s = sb("mq_s", [P, P], BF16)
        mk_s = sb("mk_s", [P, P], BF16)
        hm_s = sb("hm_s", [P, 2])

        bigb = big[:, :].bitcast(BF16)
        Qs = bigb[:, 0:16384].rearrange("p (n t s c) -> p n t s c", n=B * NP, t=T, s=SLOTS)
        Ks = bigb[:, 16384:32768].rearrange("p (n t s c) -> p n t s c", n=B * NP, t=T, s=SLOTS)
        KT = work[:, :, :, :, :].rearrange("p w b t c -> p (w b t c)").bitcast(BF16).rearrange(
            "p (r h s) -> p r h s", r=2, h=GH)
        QT = ffn_h[:, 0].bitcast(BF16).rearrange("p (n s) -> p n s", n=2)
        QmT = ffn_h[:, 1].bitcast(BF16).rearrange("p (n s) -> p n s", n=2)
        qk_01 = big[:, 0:8192].bitcast(F16).rearrange("p (r m h s) -> p r m h s", r=2, m=4, h=2)
        qk_2 = work[:, :, :, :, :].rearrange("p w b t c -> p (w b t c)").bitcast(F16).rearrange(
            "p (m h s) -> p m h s", m=4, h=2)
        Q1, K1, Q2, K2 = ([qk_01[:, 0, m], qk_01[:, 1, m], qk_2[:, m]] for m in range(4))
        YT = big[:, 8192:16384].rearrange("p (n s) -> p n s", n=NP)
        Pr1 = Pr[:, 0, 0:2, :]
        qk_raw = Pr[:, 0, 2:4, :]
        VA = Pr[:, 1, :, :].rearrange("p a s -> p (a s)")[:, 0:QK_SETS * T * 2 * VW].rearrange(
            "p (r t h c) -> p r t h c", r=QK_SETS, t=T, h=2)
        Y1 = OT[:, :].rearrange("p (t c) -> p t c", t=T)
        ws1 = sb("ws1", [P, QK_SETS, 2, P])
        prf = Pr[:, :, :, :].rearrange("p r h s -> p (r h s)")
        cosT = prf[:, 0:2048].rearrange("p (t c) -> p t c", t=T)
        sinT = prf[:, 2048:4096].rearrange("p (t c) -> p t c", t=T)
        R = prf[:, 4096:5120].rearrange("p (t c) -> p t c", t=4)
        R2 = prf[:, 5120:6144].rearrange("p (t c) -> p t c", t=4)
        raw_gu = ffn_h[:, 0, 0:2 * HID].bitcast(I32).rearrange("p (a c) -> p a c", a=2)
        raw_masks = ffn_h[:, 2, 2 * P:4 * P].rearrange("p (a c) -> p a c", a=2)
        raw_int = ffn_h[:, 2, 0:2 * P].bitcast(I64)
        raw_d = ffn_h[:, 1, 0:HID].bitcast(I32).rearrange("p (a c) -> p a c", a=HC)

        ps = ctx.enter_context(nc.psum_tensor("ps", [P, 8, 512], F32))

        def banks(b, n):
            return ps[:, b:b + n, :].rearrange("p a c -> p (a c)")

        def ubank(key):
            return 4 * (UNIT_AT[key] % 2)

        x_in, w_in, k_in = sem("x_in"), sem("w_in"), sem("k_in")
        wprep = sem("wprep")
        centred, squared, var_ready, sd_ready = sem("centred"), sem("squared"), sem("var_ready"), sem("sd_ready")
        norm_ready = sem("norm_ready")
        pe_unit, act_unit, dve_unit = sem("pe_unit"), sem("act_unit"), sem("dve_unit")
        split_done, dups_done, slots_set = sem("split_done"), sem("dups_done"), sem("slots_set")
        ring_filled, ring_act, ring_dve = sem("ring_filled"), sem("ring_act"), sem("ring_dve")
        ring_read = {"A": ring_act, "V": ring_dve}
        shift_ready, acts_laid = sem("shift_ready"), sem("acts_laid")
        v_staged, vs_set = sem("v_staged"), sem("vs_set")
        pv0, acc0_saved = sem("pv0"), sem("acc0_saved")
        pv1, acc1_saved = sem("pv1"), sem("acc1_saved")
        rows_set, w_staged = sem("rows_set"), sem("w_staged")
        wmax_ready, scale_ready, w_scaled = sem("wmax_ready"), sem("scale_ready"), sem("w_scaled")
        high_done, low_done, copy_done = sem("high_done"), sem("low_done"), sem("copy_done")
        shift1_ready = sem("shift1_ready")
        dve_step = sem("dve_step")
        pe_gate = sem("pe_gate")
        out_done = sem("out_done")

        block = ctx.enter_context(nc.Block())
        x_v = x.rearrange("(b t p) c -> p b t c", b=B, t=T)
        o_v = out.rearrange("(b t p) c -> p b t c", b=B, t=T)

        @block.sync
        def _(sp):
            for b in range(B):
                sp.dma_start(X[:, b], x_v[:, b]).then_inc(x_in, 16)
            sp.dma_start(wkqv_s[:], w_kqv).then_inc(w_in, 16)
            sp.dma_start(wo0_s[:], w_o0).then_inc(w_in, 16)
            sp.dma_start(cosT, rope_cos).then_inc(w_in, 16)
            sp.dma_start(sinT, rope_sin).then_inc(w_in, 16)
            for n, w in enumerate((w_q, w_k, w_v)):
                sp.dma_start(wqkv1[:, n, :], w).then_inc(w_in, 16)
            sp.dma_start(wo1_s[:], w_o1.rearrange("(n p) c -> p n c", p=P)).then_inc(w_in, 16)
            for b in range(B):
                sp.wait_ge(dve_unit, read_by("V", UNIT_AT[("mm", 5, b)]))
                sp.dma_start(o_v[:, b], X[:, b]).then_inc(out_done, 16)
            sp.wait_ge(out_done, 16 * B)

        W_LOADS = 8
        FREE = 2

        @block.gpsimd
        def _(pool):
            g = nc.gpsimd
            g.memset(Qs[:, :, :, 6:8, :].rearrange("p n t s c -> p (n t) (s c)"), 0.0)
            g.memset(Ks[:, :, :, 6:8, :].rearrange("p n t s c -> p (n t) (s c)"), 0.0).then_inc(slots_set, 1)
            g.memset(VS[:], 0.0).then_inc(vs_set, 1)
            pool.wait_ge(slots_set, 1)
            g.memset(Ks[:, :, :, SHIFT_SLOT, :].rearrange("p n t (h d) -> p (n t) h d", h=2)[:, :, :, 0:3],
                     1.0).then_inc(slots_set, 1)
            pool.wait_ge(vs_set, 1)
            g.memset(VS[:, :, :, :, D0:D0 + 1].rearrange("p r t h c -> p (r t h) c"), 1.0).then_inc(vs_set, 1)

            def stage_values(group, r):
                g.tensor_copy(VS[:, r, :, :, 0:D0],
                              V0[:, group].rearrange("p t (h d) -> p t h d", h=GH)).then_inc(v_staged, 1)

            pool.wait_ge(vs_set, 2)
            pool.wait_ge(act_unit, read_by("A", UNIT_AT[("qkv", B - 1, 1)]))
            stage_values(0, 0)
            stage_values(1, 1)
            with pool.Fori(1, G // 2) as i:
                for r in range(2):
                    pool.wait_ge(pv0, T * (2 * i + r - 1) + FREE)
                    stage_values(2 * i + r, r)

            pool.wait_ge(ring_filled, GROUP_LAST.filled(len(GROUP_LAST.steps) - 1, 0))
            for r in range(QK_SETS):
                if r == QK_SETS - 1:
                    pool.wait_ge(pe_unit, filled(("turn", 4, B - 1)))
                g.memset(Q2[r][D1:P], 0.0)
                g.memset(K2[r][D1:P], 0.0).then_inc(rows_set, 1)
                pool.wait_ge(rows_set, 3 * r + 1)
                g.memset(K2[r][D1:D1 + 2], SHIFT_LOW).then_inc(rows_set, 1)
                pool.wait_ge(rows_set, 3 * r + 2)
                g.memset(K2[r][D1:D1 + 1], SHIFT_TOP).then_inc(rows_set, 1)
                pool.wait_ge(rows_set, 3 * r + 3)
            pool.wait_ge(pv0, T * G + FREE)
            g.memset(VA[:, :, :, :, D1:D1 + 1].rearrange("p r t h c -> p (r t h) c"), 1.0).then_inc(rows_set, 1)

            def stage_weights(n, r):
                g.tensor_copy(ws1[:, r], wqkv1[:, 0:2, bass.ds(n * P, P)]).then_inc(w_staged, 1)

            def low_parts(first, start):
                r, pair = first % QK_SETS, first + start
                pool.wait_ge(high_done, 2 * pair + 1)
                pool.wait_ge(w_staged, pair + min(2, B * NP - first))
                for n, (low, high) in enumerate(((Q2[r][0:D1], Q1[r]), (K1[r][D1:P], K1[r]))):
                    if n:
                        pool.wait_ge(high_done, 2 * pair + 2)
                    for head in range(2):
                        rows = slice(head * D1, (head + 1) * D1)
                        if n or head:
                            pool.wait_ge(low_done, 4 * pair + 2 * n + head)
                        if n and head:
                            pool.wait_ge(copy_done, 2 * pair + 2)
                        g.tensor_tensor(low[:, head], qk_raw[rows, n], high[rows, head],
                                        ALU.subtract).then_inc(low_done, 1)
                if first + 2 < B * NP:
                    pool.wait_ge(low_done, 4 * pair + 4)
                    stage_weights((first + 2) % NP + start, (first + 2) % QK_SETS)

            pool.wait_ge(w_scaled, 1)
            pool.wait_ge(rows_set, 3 * QK_SETS + 1)
            stage_weights(0, 0)
            stage_weights(1, 1)
            for b in range(B):
                with pool.Fori(0, (NP - 2) // QK_SETS) as i:
                    for r in range(QK_SETS):
                        low_parts(b * NP + r, QK_SETS * i)
                for n in range(NP - 2, NP):
                    low_parts(b * NP + n, 0)

        @block.scalar
        def _(act):
            a = nc.scalar
            for n, (dst, src) in enumerate(((raw_int, w_int), (wsc_s[:], w_scale), (bias_s[:], bias),
                                            (id_s[:], ident), (raw_masks[:, 0], mask_q),
                                            (raw_masks[:, 1], mask_k), (hm_s[:], head_mask),
                                            (raw_gu[:, 0, :], w_gate), (raw_gu[:, 1, :], w_up),
                                            (raw_d, w_down.rearrange("(n p) c -> p n c", p=P)))):
                act.dma_start(dst, src).then_inc(k_in, 16)

            def unit(key):
                act.wait_ge(pe_unit, filled(key))

            def ln_square(s, b):
                act.wait_ge(centred, B * s + b + 1)
                a.activation(W[:, b], D[:, b], ACT.Square).then_inc(squared, 1)

            def ln_root(s, b):
                act.wait_ge(var_ready, B * s + b + 1)
                a.activation(stats[:, 3, b, :], stats[:, 2, b, :], ACT.Sqrt).then_inc(sd_ready, 1)

            def turned(s, b, dst, bf=False):
                key = ("turn", s, b)
                unit(key)
                src = banks(ubank(key), 1).bitcast(BF16) if bf else banks(ubank(key), 2)
                a.activation(dst, src, ACT.Copy).then_inc(act_unit, 1)

            def norm(s):
                for b in range(B):
                    ln_square(s, b)
                for b in range(B):
                    ln_root(s, b)

            def gated(s):
                norm(s)
                for b in range(B):
                    turned(s, b, XT[:, b])
                    for c in range(HC):
                        key = ("up", s, b, c)
                        unit(key)
                        last = ("up", s, b, c - 2) if c >= 2 else ("up", s, b - 1, c + 1) if b else None
                        if last:
                            act.wait_ge(dve_unit, read_by("V", UNIT_AT[last]))
                        a.activation(ffn_g[:, c % 2 if b == 0 else (c + 1) % 2], banks(ubank(key), 2),
                                     ACT.Silu).then_inc(act_unit, 1)

            norm(0)
            for b in range(B):
                turned(0, b, XQT[:, b], True)
            norm(1)
            for b in range(B):
                turned(1, b, XT[:, b])
                for half in range(2):
                    key = ("qkv", b, half)
                    unit(key)
                    t0 = 4 * half
                    src = ps[:, ubank(key):ubank(key) + 4, 2 * P:3 * P]
                    a.activation(V0[:, b * GB:(b + 1) * GB, t0:t0 + 4, :].rearrange("p g t c -> p t g c"),
                                 src.rearrange("p t (g c) -> p t g c", g=GB), ACT.Copy).then_inc(act_unit, 1)
                    act.wait_ge(split_done, 2 * b + half + 1)
                    for stack, parts in ((Qs, Q_PARTS), (Ks, K_PARTS)):
                        for slot, part in enumerate(parts):
                            if slot != parts.index(part):
                                view = stack[:, b * NP:(b + 1) * NP, t0:t0 + 4]
                                ins = a.activation(view[:, :, :, slot, :], view[:, :, :, parts.index(part), :],
                                                   ACT.Copy)
                    ins.then_inc(dups_done, 1)

            def group_turn(turn, i, g0):
                base, par = g0
                done = 0
                for k, (kind, ahead, arg, reader) in enumerate(turn.steps):
                    if kind == "heads":
                        done += 1
                        continue
                    if reader != "A":
                        continue
                    slot = banks(turn.bank(k), 2)
                    r = (par + done + ahead) % 2
                    if kind == "k":
                        act.wait_ge(ring_filled, turn.filled(k, i))
                        src = slot.bitcast(BF16).rearrange("p (n s) -> p n s", n=2)
                        for hh in range(2):
                            ins = a.activation(KT[:, r, hh::2, :], src, ACT.Copy, scale=hm_s[:, hh:hh + 1])
                        ins.then_inc(ring_act, 1)
                    if kind == "exp":
                        t, j, n = arg
                        w = (T - t) * P
                        if j == 0:
                            act.wait_ge(pv0, T * (base + done) + t + 1)
                        act.wait_ge(ring_filled, turn.filled(k, i))
                        src = slot.rearrange("p (n c) -> p n c", n=n)[:, :, 0:w]
                        a.activation(Pr[:, t % 2, j:j + n, 0:w], src, ACT.Exp, scale=SCALE0).then_inc(ring_act, 1)
                        if t == T - 1:
                            act.wait_ge(pv0, T * (base + done + 1) + FREE)
                            a.activation(OT[:], banks(6, 2), ACT.Copy).then_inc(acc0_saved, 1)

            act.wait_ge(k_in, 16 * 10)
            group_turn(GROUP_FIRST, 0, (0, 0))
            with act.Fori(0, GROUP_LOOP.times) as i:
                group_turn(GROUP_LOOP, i, (2 * i, 0))
            group_turn(GROUP_LAST, 0, (G - 2, 0))

            act.wait_ge(ring_dve, GROUP_LAST.read("V", len(GROUP_LAST.steps) - 1, 0))
            for b in range(B):
                a.activation(D[:, b].rearrange("p t (g c) -> p t g c", g=GB),
                             acts[:, b * GB:(b + 1) * GB].rearrange("p g t c -> p t g c"), ACT.Copy).then_inc(acts_laid, 1)
            for b in range(B):
                key = ("acts", b)
                unit(key)
                a.activation(XT[:, b], banks(ubank(key), 2), ACT.Copy).then_inc(act_unit, 1)
            act.wait_ge(scale_ready, 1)
            a.activation(wqkv1[:, 0], wqkv1[:, 0], ACT.Copy, scale=qk_scale[:, 0:1])
            a.activation(wqkv1[:, 1], wqkv1[:, 1], ACT.Copy, scale=qk_scale[:, 1:2]).then_inc(w_scaled, 1)
            norm(2)
            for b in range(B):
                turned(2, b, XQT[:, b], True)
            gated(3)
            norm(4)
            for b in range(B):
                turned(4, b, XT[:, b])

            def pair_turn(turn, i, first, start):
                done = 0
                for k, (kind, h, t, reader) in enumerate(turn.steps):
                    slot = banks(turn.bank(k), 2)
                    if kind in ("proj_q", "proj_k"):
                        n, pair = int(kind == "proj_k"), first + start + done + h
                        if first + done + h > 0:
                            act.wait_ge(low_done, 4 * pair - 2 + 2 * n)
                        act.wait_ge(ring_filled, turn.filled(k, i))
                        a.activation(qk_raw[:, n], slot, ACT.Copy).then_inc(ring_act, 1)
                    if kind == "proj_v":
                        act.wait_ge(ring_filled, turn.filled(k, i))
                        a.activation(VA[:, (first + done + h) % QK_SETS, :, :, 0:D1],
                                     slot.rearrange("p (t h c) -> p t h c", t=T, h=2), ACT.Copy).then_inc(ring_act, 1)
                    if kind == "yT":
                        act.wait_ge(ring_filled, turn.filled(k, i))
                        a.activation(YT[:, bass.ds((first + done) % NP + start, 1),
                                        512 * h:512 * h + 512].rearrange("p n s -> p (n s)"),
                                     slot[:, 0:512], ACT.Copy).then_inc(ring_act, 1)
                    if kind == "shift":
                        act.wait_ge(ring_filled, turn.filled(k, i))
                        a.activation(Q2[(first + done + 1 - h) % QK_SETS][D1:D1 + 2, h],
                                     slot.bitcast(F16)[D1:D1 + 2, 0:S], ACT.Copy).then_inc(ring_act, 1)
                    if kind == "exp":
                        w = (T - t) * P
                        act.wait_ge(pv1, T * (2 * (first + start + done) + h) + t + 1)
                        act.wait_ge(ring_filled, turn.filled(k, i))
                        a.activation(Pr1[:, t % 2, 0:w], slot[:, 0:w], ACT.Exp,
                                     scale=exp_scale[:, 0:1]).then_inc(ring_act, 1)
                    if kind == "yT" and h == 1:
                        done += 1

            pair_turn(PAIR_FIRST, 0, -1, 0)
            for b, (loop, last) in enumerate(PAIR_TURNS):
                with act.Fori(0, loop.times) as i:
                    pair_turn(loop, i, b * NP, QK_SETS * i)
                pair_turn(last, 0, (b + 1) * NP - 2, 0)
            gated(5)

        @block.vector
        def _(dve):
            v = nc.vector
            steps = [0, None, 0]

            def link(ins):
                ins.then_inc(dve_step, 1)
                steps[0] += 1
                dve.wait_ge(dve_step, steps[0] if steps[1] is None else steps[0] + steps[1] * steps[2])

            def small(ap):
                return ap.unsqueeze(2).to_broadcast([P, T, P])

            v.memset(ones_s[:], 1.0)
            v.sem_inc(pv0, FREE)
            v.sem_inc(pv1, FREE)
            dve.wait_ge(x_in, 16 * B)

            def centre(s, b):
                link(v.reduce_sum(stats[:, 0, b, :], X[:, b], AX.X))
                link(v.tensor_scalar(stats[:, 1, b, :], stats[:, 0, b, :], 1.0 / P, None, ALU.mult))
                v.tensor_tensor(D[:, b], X[:, b], small(stats[:, 1, b, :]), ALU.subtract).then_inc(centred, 1)

            def variance(s, b):
                dve.wait_ge(squared, B * s + b + 1)
                link(v.reduce_sum(stats[:, 0, b, :], W[:, b], AX.X))
                v.tensor_scalar(stats[:, 2, b, :], stats[:, 0, b, :], 1.0 / P, LN_EPS, ALU.mult,
                                ALU.add).then_inc(var_ready, 1)

            def normalise(s, b):
                dve.wait_ge(sd_ready, B * s + b + 1)
                r, t, var = stats[:, 4, b, :], stats[:, 5, b, :], stats[:, 2, b, :]
                link(v.reciprocal(r, stats[:, 3, b, :]))
                link(v.tensor_tensor(t, r, r, ALU.mult))
                link(v.tensor_tensor(t, t, var, ALU.mult))
                link(v.tensor_scalar(t, t, -0.5, 1.5, ALU.mult, ALU.add))
                link(v.tensor_tensor(r, r, t, ALU.mult))
                return v.tensor_tensor(D[:, b], D[:, b], small(r), ALU.mult)

            def norm(s, to_turn=True):
                for b in range(B):
                    centre(s, b)
                for b in range(B):
                    variance(s, b)
                for b in range(B):
                    ins = normalise(s, b)
                    if to_turn:
                        ins.then_inc(norm_ready, 1)
                    else:
                        link(ins)

            def int_ffn(s):
                norm(s, False)
                for b in range(B):
                    amax, xs, inv = stats[:, 6, b, :], stats[:, 7, b, :], stats[:, 8, b, :]
                    link(v.tensor_reduce(amax, D[:, b], AX.X, ALU.max, apply_absolute_value=True))
                    link(v.tensor_scalar(xs, amax, Q_EPS, 1.0 / 127.0, ALU.max, ALU.mult))
                    link(v.reciprocal(inv, xs))
                    link(v.tensor_tensor(W[:, b], D[:, b], small(inv), ALU.mult))
                    link(v.tensor_scalar(W[:, b], W[:, b], MAGIC, MAGIC, ALU.add, ALU.subtract))
                    v.tensor_scalar(XQ[:, b], W[:, b], 127.0, -128.0, ALU.min, ALU.max).then_inc(norm_ready, 1)
                for b in range(B):
                    key = ("mm", s, b)
                    dve.wait_ge(pe_unit, filled(key))
                    acc = banks(ubank(key), 2).rearrange("p (t c) -> p t c", t=T)
                    for t in range(T):
                        ins = v.scalar_tensor_tensor(W[:, b, t], acc[:, t], stats[:, 7, b, t:t + 1], wsc_s[:],
                                                     ALU.mult, ALU.mult)
                    ins.then_inc(dve_unit, 1)
                    dve.wait_ge(dve_unit, read_by("V", UNIT_AT[key]))
                    link(v.tensor_tensor(W[:, b], W[:, b], bias_s[:].unsqueeze(1).to_broadcast([P, T, P]), ALU.add))
                    link(v.tensor_tensor(X[:, b], X[:, b], W[:, b], ALU.add))

            def add_to_x(key, b, factor):
                dve.wait_ge(pe_unit, filled(key))
                acc = banks(ubank(key), 2).rearrange("p (t c) -> p t c", t=T)
                v.scalar_tensor_tensor(X[:, b], acc, factor, X[:, b], ALU.mult, ALU.add).then_inc(dve_unit, 1)
                dve.wait_ge(dve_unit, read_by("V", UNIT_AT[key]))

            def gated(s):
                norm(s)
                for b in range(B):
                    for c in range(HC):
                        key = ("up", s, b, c)
                        dve.wait_ge(act_unit, read_by("A", UNIT_AT[key]))
                        dve.wait_ge(pe_unit, filled(key))
                        v.tensor_tensor(ffn_h[:, c], ffn_g[:, c % 2 if b == 0 else (c + 1) % 2],
                                        banks(ubank(key) + 2, 2), ALU.mult).then_inc(dve_unit, 1)
                    add_to_x(("mm", s, b), b, 0.5)

            dve.wait_ge(k_in, 16 * 10)
            v.tensor_copy(idb_s[:], id_s[:])
            v.tensor_copy(idh_s[:], id_s[:])
            v.tensor_copy(mq_s[:], raw_masks[:, 0])
            v.tensor_copy(mk_s[:], raw_masks[:, 1])
            v.tensor_copy(wint_s[:], raw_int.bitcast(I32).rearrange("p (c two) -> p c two", two=2)[:, :, 0]).then_inc(wprep, 1)
            link(v.tensor_scalar(wsc_s[:], wsc_s[:], 0.5, None, ALU.mult))
            link(v.tensor_scalar(bias_s[:], bias_s[:], 0.5, None, ALU.mult))
            v.tensor_scalar(wg_s[:], raw_gu, W_SCALE, None, ALU.mult).then_inc(wprep, 1)
            link(v.tensor_scalar(wd_s[:], raw_d, W_SCALE, None, ALU.mult))
            int_ffn(0)

            norm(1)
            dve.wait_ge(w_in, 16 * W_LOADS)
            for b in range(B):
                for half in range(2):
                    key = ("qkv", b, half)
                    dve.wait_ge(pe_unit, filled(key))
                    dve.wait_ge(act_unit, read_by("A", UNIT_AT[key]))
                    t0 = 4 * half
                    kq = ps[:, ubank(key):ubank(key) + 4, 0:2 * P]
                    pairs = kq.rearrange("p t (n two) -> p t n two", two=2)
                    sp = sinT[:, t0:t0 + 4].rearrange("p t (n two) -> p t n two", two=2)
                    r2 = R2.rearrange("p t (n two) -> p t n two", two=2)
                    v.tensor_tensor(R, kq, cosT[:, t0:t0 + 4], ALU.mult)
                    v.tensor_tensor(r2[:, :, :, 0], pairs[:, :, :, 1], sp[:, :, :, 0], ALU.mult)
                    v.tensor_tensor(r2[:, :, :, 1], pairs[:, :, :, 0], sp[:, :, :, 1], ALU.mult).then_inc(dve_unit, 1)
                    dve.wait_ge(dve_unit, read_by("V", UNIT_AT[key]))
                    link(v.tensor_tensor(R, R, R2, ALU.add))
                    for n, (stack, parts) in enumerate(((Ks, K_PARTS), (Qs, Q_PARTS))):
                        rest = R[:, :, n * P:(n + 1) * P].rearrange("p t (n c) -> p t n c", n=NP)
                        view = stack[:, b * NP:(b + 1) * NP, t0:t0 + 4]
                        for part in range(3):
                            dst = view[:, :, :, parts.index(part), :].rearrange("p n t c -> p t n c")
                            ins = v.tensor_copy(dst, rest)
                            if part < 2:
                                link(ins)
                                link(v.tensor_tensor(rest, rest, dst, ALU.subtract))
                    ins.then_inc(split_done, 1)

            v.tensor_reduce(wmax[:, 0:1], wqkv1[:, 0], AX.X, ALU.max, apply_absolute_value=True)
            v.tensor_reduce(wmax[:, 1:2], wqkv1[:, 1], AX.X, ALU.max,
                            apply_absolute_value=True).then_inc(wmax_ready, 1)

            def group_turn(turn, i, base, next_group):
                done = 0
                for k, (kind, ahead, arg, reader) in enumerate(turn.steps):
                    if reader != "V":
                        continue
                    dve.wait_ge(ring_filled, turn.filled(k, i))
                    slot = banks(turn.bank(k), 2)
                    if kind == "max":
                        t, j, n = arg
                        src = slot.rearrange("p (n c) -> p n c", n=n)[:, :, 0:(t + 1) * P]
                        v.tensor_reduce(mx0[:, t, j:j + n], src, AX.X, ALU.max, negate=True).then_inc(ring_dve, 1)
                        if (t, j + n) == (T - 1, GH):
                            dve.wait_ge(ring_dve, turn.read("V", k, i))
                            view = Qs[:, bass.ds(2 * (next_group + done), 2), :, SHIFT_SLOT, :]
                            view = view.rearrange("p a t (h d) -> p a t h d", h=2)
                            by_pair = [m.rearrange("p t (a h) -> p a t h", a=2) for m in (mx0[:], mr0[:, 0], mr0[:, 1])]
                            link(v.tensor_copy(view[:, :, :, :, 0], by_pair[0]))
                            link(v.tensor_tensor(by_pair[1], by_pair[0], view[:, :, :, :, 0], ALU.subtract))
                            link(v.tensor_copy(view[:, :, :, :, 1], by_pair[1]))
                            link(v.tensor_tensor(by_pair[2], by_pair[1], view[:, :, :, :, 1], ALU.subtract))
                            v.tensor_copy(view[:, :, :, :, 2], by_pair[2]).then_inc(shift_ready, 1)
                    if kind in ("q", "shifted_q"):
                        dst = QT if kind == "q" else QmT
                        v.tensor_copy(dst[:], slot.bitcast(BF16).rearrange("p (n s) -> p n s", n=2)).then_inc(ring_dve, 1)
                    if kind == "heads":
                        src = slot.rearrange("p (t h c) -> p t h c", t=T, h=GH)
                        link(v.reciprocal(rs0[:], src[:, :, :, D0]))
                        v.tensor_tensor(acts[:, base + done].rearrange("p t (h d) -> p t h d", h=GH),
                                        src[:, :, :, 0:D0], rs0[:].unsqueeze(3).to_broadcast([P, T, GH, D0]),
                                        ALU.mult).then_inc(ring_dve, 1)
                        done += 1

            def looped(times, links, body):
                start = steps[0]
                with dve.Fori(0, times) as i:
                    steps[1:] = [i, links]
                    body(i)
                assert steps[0] == start + links, (steps[0] - start, links)
                steps[:] = [start + links * times, None, 0]

            group_turn(GROUP_FIRST, 0, 0, 0)
            looped(GROUP_LOOP.times, 10, lambda i: group_turn(GROUP_LOOP, i, 2 * i, 2 * i + 1))
            group_turn(GROUP_LAST, 0, G - 2, G - 1)
            for b in range(B):
                add_to_x(("mm", 1, b), b, 1.0)
            dve.wait_ge(pe_unit, filled(("wscale",)))
            v.tensor_scalar(wsum[:], ps[:, ubank(("wscale",)), 0:2], 1e-15, None, ALU.max).then_inc(dve_unit, 1)
            dve.wait_ge(dve_unit, read_by("V", UNIT_AT[("wscale",)]))
            link(v.reciprocal(wsum[:], wsum[:]))
            link(v.tensor_scalar(wsum[:], wsum[:], QK_BOUND / float(P) ** 0.5, None, ALU.mult))
            link(v.tensor_scalar(qk_scale[:].bitcast(I32), wsum[:].bitcast(I32), 0x7F800000, None,
                                 ALU.bitwise_and))
            link(v.tensor_tensor(exp_scale[:], qk_scale[:, 0:1], qk_scale[:, 1:2], ALU.mult))
            link(v.reciprocal(exp_scale[:], exp_scale[:]))
            link(v.tensor_scalar(exp_scale[:], exp_scale[:], SCALE1, None, ALU.mult))
            v.sem_inc(scale_ready, 1)
            int_ffn(2)
            gated(3)
            norm(4)

            def pair_turn(turn, i, first, start):
                done = 0
                owed = False
                last_max = None

                def shift(k, h):
                    dve.wait_ge(ring_dve, turn.read("V", k, i))
                    link(v.tensor_scalar(mx1[:, h], mx1[:, h], 1 / SHIFT_TOP, None, ALU.mult))
                    link(v.tensor_copy(sh1[:, h, :, 0], mx1[:, h]))
                    link(v.tensor_tensor(mx1[:, h], mx1[:, h], sh1[:, h, :, 0], ALU.subtract))
                    v.tensor_scalar(sh1[:, h, :, 1], mx1[:, h], SHIFT_TOP / SHIFT_LOW, None,
                                    ALU.mult).then_inc(shift1_ready, 1)

                def weighted(h):
                    n = 2 * (first + start + done) + h
                    dve.wait_ge(pv1, T * (n + 1) + FREE)
                    acc = ps[:, 6:8, 0:4 * VW].rearrange("p a (t c) -> p a t c", t=4)
                    rs = rs1[:, h].rearrange("p (a t) -> p a t", a=2)
                    link(v.reciprocal(rs, acc[:, :, :, D1]))
                    v.tensor_tensor(Y1[:, :, h * D1:(h + 1) * D1].rearrange("p (a t) c -> p a t c", a=2),
                                    acc[:, :, :, 0:D1], rs.unsqueeze(3).to_broadcast([P, 2, 4, D1]),
                                    ALU.mult).then_inc(acc1_saved, 1)

                for k, (kind, h, t, reader) in enumerate(turn.steps):
                    if kind == "exp" and (h, t) == (1, 1):
                        weighted(0)
                        owed = True
                    if owed and kind in ("proj_v", "yT"):
                        weighted(1)
                        owed = False
                    if last_max is not None and kind in ("proj_v", "yT"):
                        shift(last_max, 1)
                        last_max = None
                    if kind in ("proj_q", "proj_k"):
                        n = 2 * (first + start + done + h) + (2 if kind == "proj_k" else 1)
                        r = (first + done + h) % QK_SETS
                        dve.wait_ge(ring_act, turn.read("A", k, i))
                        stack, raw = (Q1[r], qk_raw[:, 0]) if kind == "proj_q" else (K1[r], qk_raw[:, 1])
                        v.tensor_copy(stack[0:D1, 0], raw[0:D1])
                        v.tensor_copy(stack[D1:P, 1], raw[D1:P]).then_inc(high_done, 1)
                        dve.wait_ge(high_done, n)
                        if kind == "proj_q":
                            v.tensor_copy(stack[D1:P, 0], stack[0:D1, 0])
                        else:
                            v.tensor_copy(K2[r][0:D1, 0], stack[0:D1, 0])
                            v.tensor_copy(K2[r][0:D1, 1], stack[D1:P, 1])
                        v.tensor_copy(stack[0:D1, 1], stack[D1:P, 1]).then_inc(copy_done, 1)
                    if reader == "V":
                        dve.wait_ge(ring_filled, turn.filled(k, i))
                        slot = banks(turn.bank(k), 2)
                        if kind == "max":
                            v.tensor_reduce(mx1[:, h, t:t + 1], slot[:, 0:(t + 1) * P], AX.X, ALU.max,
                                            negate=True).then_inc(ring_dve, 1)
                            if (h, t) == (1, 1):
                                shift(k, 0)
                            if (h, t) == (1, T - 1):
                                last_max = k
                        if kind == "wo":
                            half = X[:, first // NP]
                            v.tensor_tensor(half, slot.rearrange("p (t c) -> p t c", t=T), half,
                                            ALU.add).then_inc(ring_dve, 1)
                    if kind == "yT" and h == 1:
                        done += 1

            pair_turn(PAIR_FIRST, 0, -1, 0)
            for b, (loop, last) in enumerate(PAIR_TURNS):
                looped(loop.times, 8 * QK_SETS, lambda i: pair_turn(loop, i, b * NP, QK_SETS * i))
                pair_turn(last, 0, (b + 1) * NP - 2, 0)
            dve.wait_ge(ring_dve, last.read("V", len(last.steps) - 1, 0))
            gated(5)

        @block.tensor
        def _(pe):
            te = nc.tensor

            def unit(key, ring=None):
                n = UNIT_AT[key]
                if n >= 2:
                    for e, s in (("A", act_unit), ("V", dve_unit)):
                        if e in UNITS[n - 2][1]:
                            pe.wait_ge(s, read_by(e, n - 2))
                if ring:
                    for e in "AV":
                        pe.wait_ge(ring_read[e], ring.read(e, len(ring.steps) - 1, 0))
                return ubank(key)

            def turn_half(key, src, ident_ap, bf=False, ring=None):
                b0 = unit(key, ring)
                for t in range(T):
                    if bf:
                        dst = banks(b0, 1).bitcast(BF16)[:, t * P:(t + 1) * P]
                    else:
                        dst = banks(b0, 2)[:, t * P:(t + 1) * P]
                    ins = te.transpose(dst, src(t), ident_ap)
                ins.then_inc(pe_unit, 1)

            def int_ffn(s):
                for b in range(B):
                    pe.wait_ge(norm_ready, B * s + b + 1)
                    turn_half(("turn", s, b), lambda t: XQ[:, b, t], idb_s[:], True)
                    key = ("mm", s, b)
                    b0 = unit(key)
                    pe.wait_ge(act_unit, read_by("A", UNIT_AT[("turn", s, b)]))
                    for t in range(T):
                        ins = te.matmul(banks(b0, 2)[:, t * P:(t + 1) * P], XQT[:, b, t * P:(t + 1) * P],
                                        wint_s[:], start=True, stop=True)
                    ins.then_inc(pe_unit, 1)

            def gated(s):
                for b in range(B):
                    pe.wait_ge(norm_ready, B * s + b + 1)
                    turn_half(("turn", s, b), lambda t: D[:, b, t], id_s[:])
                    for c in range(HC):
                        key = ("up", s, b, c)
                        b0 = unit(key)
                        pe.wait_ge(act_unit, read_by("A", UNIT_AT[("turn", s, b)]))
                        for m in range(2):
                            for n in range(2):
                                ins = te.matmul(ps[:, b0 + 2 * m + n], wg_s[:, m, c * P:(c + 1) * P],
                                                XT[:, b, 512 * n:512 * n + 512], start=True, stop=True)
                        ins.then_inc(pe_unit, 1)
                    key = ("mm", s, b)
                    b0 = unit(key)
                    pe.wait_ge(dve_unit, read_by("V", UNIT_AT[("up", s, b, HC - 1)]))
                    for t in range(T):
                        for c in range(HC):
                            ins = te.matmul(banks(b0, 2)[:, t * P:(t + 1) * P], ffn_h[:, c, t * P:(t + 1) * P],
                                            wd_s[:, c], start=c == 0, stop=c == HC - 1)
                    ins.then_inc(pe_unit, 1)

            pe.wait_ge(k_in, 16 * 10)
            pe.wait_ge(wprep, 2)
            int_ffn(0)
            pe.wait_ge(w_in, 16 * W_LOADS)
            for b in range(B):
                pe.wait_ge(norm_ready, B * 1 + b + 1)
                turn_half(("turn", 1, b), lambda t: D[:, b, t], id_s[:])
                for half in range(2):
                    key = ("qkv", b, half)
                    b0 = unit(key)
                    pe.wait_ge(act_unit, read_by("A", UNIT_AT[("turn", 1, b)]))
                    for q in range(4):
                        t = 4 * half + q
                        ins = te.matmul(ps[:, b0 + q, 0:3 * P], XT[:, b, t * P:(t + 1) * P], wkqv_s[:],
                                        start=True, stop=True)
                    ins.then_inc(pe_unit, 1)

            def free_slot(turn, k, i):
                for e, count in turn.freed(k, i):
                    pe.wait_ge(ring_read[e], count)
                return banks(turn.bank(k), 2)

            def scores(slot, off, lhsT, rhs, w, mask, mask_at):
                for c in range(0, w, 512):
                    n = min(512, w - c)
                    diag = c <= mask_at < c + n
                    ins = te.matmul(slot[:, off + c:off + c + n], lhsT, rhs[:, c:c + n], start=True, stop=not diag)
                    if diag:
                        ins = te.matmul(slot[:, off + mask_at:off + mask_at + P], idb_s[:], mask[:],
                                        start=False, stop=True)
                return ins

            def group_turn(turn, i, base, par):
                done = 0
                waiting = None

                def weigh(t, read):
                    gcount = base + done
                    pe.wait_ge(ring_act, read)
                    if t == 0:
                        pe.wait_ge(acc0_saved, gcount)
                        pe.wait_ge(v_staged, gcount + 1)
                    q0 = t * P
                    for bank in range(2):
                        a0, a1 = max(q0, 512 * bank), 512 * (bank + 1)
                        if a0 >= a1:
                            continue
                        for j in range(GH):
                            ins = te.matmul(ps[32 * j:32 * j + 32, 6 + bank, a0 - 512 * bank:512],
                                            VS[:, (par + done) % 2, t, j], Pr[:, t % 2, j, a0 - q0:a1 - q0],
                                            start=t == 0, stop=t == 4 * bank + 3, tile_position=(0, 32 * j))
                    ins.then_inc(pv0, 1)

                for k, (kind, ahead, arg, reader) in enumerate(turn.steps):
                    g = base + done + ahead
                    r = (par + done + ahead) % 2
                    if kind == "exp" and arg[:2] == (0, 0):
                        last = [q for q in range(k) if turn.steps[q][0] == "shifted_q"]
                        if last:
                            pe.wait_ge(ring_dve, turn.read("V", last[-1], i))
                        else:
                            pe.wait_ge(ring_dve, turn.c0["V"] + i * turn.reads("V"))
                    if kind == "max" and arg[:2] == (0, 0):
                        last = [q for q in range(k) if turn.steps[q][0] == "q"]
                        for e in "AV":
                            if last:
                                pe.wait_ge(ring_read[e], turn.read(e, last[-1], i))
                            else:
                                pe.wait_ge(ring_read[e], turn.c0[e] + i * turn.reads(e))
                    if kind == "heads":
                        pe.wait_ge(acc0_saved, base + done + 1)
                    if kind == "shifted_q":
                        pe.wait_ge(shift_ready, g + 1)
                    slot = free_slot(turn, k, i)
                    if kind == "max":
                        t, j, n = arg
                        for q in range(n):
                            ins = scores(slot, q * (1024 // n), QT[:, (j + q) // 2, t * P:(t + 1) * P],
                                         KT[:, r, j + q], (t + 1) * P, mq_s, t * P)
                    if kind == "exp":
                        t, j, n = arg
                        for q in range(n):
                            ins = scores(slot, q * (1024 // n), KT[:, r, j + q, t * P:(t + 1) * P],
                                         QmT[:, (j + q) // 2, t * P:], (T - t) * P, mk_s, 0)
                    if kind in ("k", "q", "shifted_q"):
                        te.sem_inc(pe_gate, 1)
                        src = Ks if kind == "k" else Qs
                        dst = slot.bitcast(BF16)
                        for pair in range(2):
                            for t in range(T):
                                c = pair * S + t * P
                                rows = src[:, bass.ds(2 * g + pair, 1), t].rearrange("p n s c -> p (n s c)")
                                ins = te.transpose(dst[:, c:c + P], rows, idb_s[:])
                    if kind == "heads":
                        for t in range(T):
                            ins = te.transpose(slot[:, t * P:(t + 1) * P], OT[:, t * P:(t + 1) * P], id_s[:])
                    ins.then_inc(ring_filled, 1)
                    nxt = turn.steps[k + 1][0] if k + 1 < len(turn.steps) else None
                    if waiting and (kind == "exp" or nxt == "heads"):
                        weigh(*waiting)
                        waiting = None
                    if kind == "exp" and arg[1] + arg[2] == GH:
                        waiting = (arg[0], turn.read("A", k, i))
                        if nxt == "heads":
                            weigh(*waiting)
                            waiting = None
                    if kind == "heads":
                        done += 1

            for n in range(2):
                u = UNIT_AT[("qkv", B - 1, 1)] - n
                pe.wait_ge(act_unit, read_by("A", u))
                pe.wait_ge(dve_unit, read_by("V", u))
            pe.wait_ge(dups_done, 2 * B)
            pe.wait_ge(slots_set, 2)
            group_turn(GROUP_FIRST, 0, 0, 0)
            with pe.Fori(0, GROUP_LOOP.times) as i:
                group_turn(GROUP_LOOP, i, 2 * i, 0)
            group_turn(GROUP_LAST, 0, G - 2, 0)

            for b in range(B):
                pe.wait_ge(acts_laid, b + 1)
                turn_half(("acts", b), lambda t: D[:, b, t], id_s[:], ring=GROUP_LAST)
                key = ("mm", 1, b)
                b0 = unit(key)
                pe.wait_ge(act_unit, read_by("A", UNIT_AT[("acts", b)]))
                for t in range(T):
                    ins = te.matmul(banks(b0, 2)[:, t * P:(t + 1) * P], XT[:, b, t * P:(t + 1) * P], wo0_s[:],
                                    start=True, stop=True)
                ins.then_inc(pe_unit, 1)
            b0 = unit(("wscale",))
            pe.wait_ge(wmax_ready, 1)
            te.matmul(ps[:, b0, 0:2], ones_s[:], wmax[:], start=True, stop=True).then_inc(pe_unit, 1)
            int_ffn(2)
            gated(3)
            for b in range(B):
                pe.wait_ge(norm_ready, B * 4 + b + 1)
                turn_half(("turn", 4, b), lambda t: D[:, b, t], id_s[:])

            def pair_turn(turn, i, first, start):
                done = 0
                waiting = None

                def weigh(h, t, read, r, n):
                    pe.wait_ge(ring_act, read)
                    if t == 0:
                        pe.wait_ge(acc1_saved, n)
                    for q in range(t, T):
                        c = (q % 4) * VW
                        ins = te.matmul(ps[:, 6 + q // 4, c:c + D1 + 1], Pr1[:, t % 2, (q - t) * P:(q - t + 1) * P],
                                        VA[:, r, t, h, 0:D1 + 1], start=t == 0 and q % 4 == 0, stop=t == q,
                                        skip_group_check=True)
                    ins.then_inc(pv1, 1)

                def read_before(e, k, kinds):
                    last = [q for q in range(k) if turn.steps[q][0] in kinds]
                    if last:
                        pe.wait_ge(ring_read[e], turn.read(e, last[-1], i))
                    else:
                        pe.wait_ge(ring_read[e], turn.c0[e] + i * turn.reads(e))

                def products(kind, r, h, t, slot):
                    c0, w = (0, (t + 1) * P) if kind == "max" else (t * P, (T - t) * P)
                    at = t * P if kind == "max" else 0
                    for c in range(0, w, 512):
                        n = min(512, w - c)
                        diag = c <= at < c + n
                        tile, cols = slice(t * P, (t + 1) * P), slice(c0 + c, c0 + c + n)
                        if kind == "max":
                            ins = te.matmul(slot[:, c:c + n], Q1[r][:, h, tile], K1[r][:, h, cols],
                                            start=True, stop=not diag)
                        else:
                            te.matmul(slot[:, c:c + n], K1[r][:, h, tile], Q1[r][:, h, cols],
                                      start=True, stop=False)
                            ins = te.matmul(slot[:, c:c + n], K2[r][:, h, tile], Q2[r][:, h, cols],
                                            start=False, stop=not diag)
                        if diag:
                            ins = te.matmul(slot[:, at:at + P], idb_s[:], (mq_s if kind == "max" else mk_s)[:],
                                            start=False, stop=True)
                    return ins

                for k, (kind, h, t, reader) in enumerate(turn.steps):
                    here = (first + done) % QK_SETS
                    whole = first + start + done
                    if kind == "max" and (h, t) == (0, 0):
                        pe.wait_ge(low_done, 4 * (whole + 1) + 4)
                        pe.wait_ge(copy_done, 2 * (whole + 1) + 2)
                    if kind == "shift":
                        pe.wait_ge(shift1_ready, 2 * (whole + 1 - h) + h + 1)
                    if kind == "exp" and t == 0:
                        read_before("A", k, ("shift",))
                    if kind == "proj_q":
                        pe.wait_ge(w_staged, whole + h + 1)
                    if kind == "yT" and h == 0:
                        pe.wait_ge(acc1_saved, 2 * whole + 2)
                    slot = free_slot(turn, k, i)
                    if kind == "max":
                        ins = products(kind, (here + 1) % QK_SETS, h, t, slot)
                    if kind == "exp":
                        ins = products(kind, here, h, t, slot)
                    if kind == "shift":
                        te.sem_inc(pe_gate, 1)
                        for q in range(T):
                            ins = te.transpose(slot.bitcast(F16)[D1:D1 + 2, q * P:(q + 1) * P], sh1[:, h, q],
                                               idh_s[:])
                    if kind in ("proj_q", "proj_k"):
                        for n in range(2):
                            ins = te.matmul(slot[:, 512 * n:512 * n + 512], ws1[:, (here + h) % QK_SETS, int(kind == "proj_k")],
                                            XT[:, (first + done + h) // NP, 512 * n:512 * n + 512], start=True, stop=True)
                    if kind == "proj_v":
                        b, n = divmod(first + done + h, NP)
                        for q in range(T):
                            ins = te.matmul(slot[:, q * P:(q + 1) * P], XT[:, b, q * P:(q + 1) * P],
                                            wqkv1[:, 2, bass.ds((n + start) * P, P)], start=True, stop=True)
                    if kind == "yT":
                        for q in range(4):
                            ins = te.transpose(slot[:, q * P:(q + 1) * P], Y1[:, 4 * h + q], id_s[:])
                    if kind == "wo":
                        pe.wait_ge(ring_act, turn.read("A", k - 1, i))
                        for t in range(T):
                            for n in range(NP):
                                ins = te.matmul(slot[:, t * P:(t + 1) * P], YT[:, n, t * P:(t + 1) * P],
                                                wo1_s[:, n], start=n == 0, stop=n == NP - 1)
                    ins.then_inc(ring_filled, 1)
                    after = turn.steps[k + 1][:2] if k + 1 < len(turn.steps) else None
                    if waiting and (kind in ("exp", "proj_v") or after[0] == "yT"):
                        weigh(*waiting)
                        waiting = None
                    if kind == "exp":
                        waiting = (h, t, turn.read("A", k, i), here, 2 * whole + h)
                        if after == ("yT", 0):
                            weigh(*waiting)
                            waiting = None
                    if kind == "yT" and h == 1:
                        done += 1

            for n in range(2):
                pe.wait_ge(act_unit, read_by("A", UNIT_AT[("turn", 4, B - 1)] - n))
            pair_turn(PAIR_FIRST, 0, -1, 0)
            pe.wait_ge(rows_set, 3 * QK_SETS + 1)
            for b, (loop, last) in enumerate(PAIR_TURNS):
                with pe.Fori(0, loop.times) as i:
                    pair_turn(loop, i, b * NP, QK_SETS * i)
                pair_turn(last, 0, (b + 1) * NP - 2, 0)
            gated(5)


def _constants():
    import numpy as np

    eye = np.eye(P, dtype=np.float32)
    row, col = np.arange(P)[:, None], np.arange(P)[None, :]
    inv_freq = np.float32(1.0) / np.float32(10000.0) ** (np.arange(0, D0, 2, dtype=np.float32) / np.float32(D0))
    ang = np.arange(S, dtype=np.float32)[:, None] * inv_freq[None, :]
    cos = np.tile(np.repeat(np.cos(ang), 2, axis=1), (1, 2 * H))
    sin = np.repeat(np.sin(ang), 2, axis=1)
    sin[:, 0::2] *= -1
    sin = np.tile(sin, (1, 2 * H))
    by_tile = lambda a: np.ascontiguousarray(a.reshape(T, P, -1).transpose(1, 0, 2)).astype(np.float32)
    hh = (np.arange(P) // D0) % 2
    return {
        "ident": eye,
        "mask_q": np.where(col > row, np.float32(-1e30), np.float32(0)),
        "mask_k": np.where(col < row, np.float32(-1e30), np.float32(0)),
        "head_mask": np.stack([hh == 0, hh == 1], axis=1).astype(np.float32),
        "rope_cos": by_tile(cos),
        "rope_sin": by_tile(sin),
    }


def kernel(L0_attn_X, L0_attn_W_KQV, L0_attn_W_O, L0_ffn_weight_q, L0_ffn_weight_scale, L0_ffn_bias,
           L1_attn_w_q, L1_attn_w_k, L1_attn_w_v, L1_attn_w_o, L1_ffn_w_gate, L1_ffn_w_up, L1_ffn_w_down):
    import numpy as np
    import concourse.bacc as bacc
    from concourse.bass_utils import run_bass_kernel_spmd

    def lay(a):
        return np.ascontiguousarray(a)

    arrays = {
        "x": lay(L0_attn_X).reshape(B * S, P),
        "w_kqv": lay(np.asarray(L0_attn_W_KQV).T),
        "w_o0": lay(np.asarray(L0_attn_W_O).T),
        "w_int": lay(np.asarray(L0_ffn_weight_q).T).astype(np.int64),
        "w_scale": lay(np.broadcast_to(np.asarray(L0_ffn_weight_scale), (P, P))),
        "bias": lay(np.broadcast_to(np.asarray(L0_ffn_bias), (P, P))),
        "w_q": lay(np.asarray(L1_attn_w_q).reshape(H * D1, P).T),
        "w_k": lay(np.asarray(L1_attn_w_k).reshape(H * D1, P).T),
        "w_v": lay(np.asarray(L1_attn_w_v).reshape(H * D1, P).T),
        "w_o1": lay(L1_attn_w_o),
        "w_gate": lay(np.asarray(L1_ffn_w_gate).T),
        "w_up": lay(np.asarray(L1_ffn_w_up).T),
        "w_down": lay(np.asarray(L1_ffn_w_down).T),
    }
    arrays.update(_constants())
    nc = bacc.Bacc("TRN2", target_bir_lowering=False, num_devices=1)
    args = [nc.dram_tensor(f"in_{n}_dram", a.shape, mybir.dt.from_np(a.dtype), kind="ExternalInput").ap()
            for n, a in arrays.items()]
    args.append(nc.dram_tensor("out_0_dram", (B * S, P), F32, kind="ExternalOutput").ap())
    macaron_block_kernel(nc, *args)
    r = run_bass_kernel_spmd(nc, [{f"in_{n}_dram": a for n, a in arrays.items()}], core_ids=[0])
    return r.results[0]["out_0_dram"].reshape(B, S, P)
```

```python
from contextlib import ExitStack

import concourse.bass as bass
from concourse import mybir

ALU = mybir.AluOpType
ACT = mybir.ActivationFunctionType
AX = mybir.AxisListType
F32 = mybir.dt.float32
BF16 = mybir.dt.bfloat16
F16 = mybir.dt.float16
I32 = mybir.dt.int32
I64 = mybir.dt.int64

P = 128
B = 2
S = 1024
T = S // P
H = 16
D0 = P // H
D1 = 64
HID = 384
HC = HID // P
SLOTS = 8
GH = 4
G = B * H // GH
GB = H // GH
SHIFT_TOP, SHIFT_LOW = 2.0**14, 2.0**3
QK_BOUND = 4096.0
NP = H // 2
LN_EPS = 1e-5
Q_EPS = 1e-6
MAGIC = 1.5 * 2.0**23
SCALE0 = float(D0) ** -0.5
SCALE1 = float(D1) ** -0.5
W_SCALE = 1.0 / 127.0
RING = 3

Q_PARTS = (0, 0, 1, 1, 0, 2)
K_PARTS = (0, 1, 0, 1, 2, 0)
SHIFT_SLOT = 6


GATED = ([("turn", 0, None), ("up", 0, 0), ("turn", 1, None)] + [("up", 0, c) for c in range(1, HC)]
         + [("up", 1, 0), ("mm", 0, None)] + [("up", 1, c) for c in range(1, HC)] + [("mm", 1, None)])


def plan_units():
    units = []

    def int_ffn(s):
        for b in range(B):
            units.append((("turn", s, b), "A"))
            units.append((("mm", s, b), "V"))

    def gated_ffn(s):
        for kind, b, c in GATED:
            key = (kind, s, b, c) if kind == "up" else (kind, s, b)
            units.append((key, {"turn": "A", "up": "AV", "mm": "V"}[kind]))

    int_ffn(0)
    for b in range(B):
        units.append((("turn", 1, b), "A"))
    for b in range(B):
        for half in range(2):
            units.append((("qkv", b, half), "AV"))
    for b in range(B):
        units.append((("acts", b), "A"))
    units.append((("wscale",), "V"))
    for b in range(B):
        units.append((("mm", 1, b), "V"))
    int_ffn(2)
    gated_ffn(3)
    for b in range(B):
        units.append((("turn", 4, b), "A"))
    gated_ffn(5)
    return units


UNITS = plan_units()
UNIT_AT = {key: n for n, (key, _) in enumerate(UNITS)}


def filled(key):
    return UNIT_AT[key] + 1


def read_by(engine, n):
    return sum(engine in who for _, who in UNITS[: n + 1])


def grouped(widths, heads):
    steps = []
    for t, w in widths:
        n = min(heads, 1 if w > 512 else 2 if w > 256 else 4)
        steps += [(t, j, n) for j in range(0, heads, n)]
    return steps


MAX_WIDTHS = [(t, (t + 1) * P) for t in range(T)]
EXP_WIDTHS = [(t, (T - t) * P) for t in range(T)]
MAX_STEPS, EXP_STEPS = grouped(MAX_WIDTHS, GH), grouped(EXP_WIDTHS, GH)
PAIR_MAXES, PAIR_EXPS = grouped(MAX_WIDTHS, 2), grouped(EXP_WIDTHS, 2)


KT_AT = (0, 3)
AHEAD = 4


def group_steps(exps, maxes, turn_after):
    steps = []
    due = list(MAX_STEPS) if maxes else []
    for n, e in enumerate(EXP_STEPS):
        if exps:
            steps.append(("exp", 0, e, "A"))
        for _ in range(2 if 0 < n <= AHEAD else 1):
            if due:
                steps.append(("max", 1, due.pop(0), "V"))
        if turn_after and n in KT_AT:
            steps.append(("k", 2, KT_AT.index(n), "A"))
    if maxes:
        steps.append(("shifted_q", 1, None, "V"))
    if turn_after:
        steps.append(("q", 2, None, "V"))
    if exps:
        steps.append(("heads", 0, None, "V"))
    return steps


PROJ_AT = {3: "proj_q", 5: "proj_k", 12: "proj_v"}
MAX_FROM, MAX_EACH = 6, 2


def pair_steps(exps, maxes, project):
    steps = []
    due = [("max", 1, m, "V") for m in PAIR_MAXES] if maxes else []
    for n, e in enumerate(PAIR_EXPS):
        if exps:
            steps.append(("exp", 0, e, "A"))
        if n >= MAX_FROM:
            steps += due[:MAX_EACH]
            due = due[MAX_EACH:]
        if project and n in PROJ_AT:
            steps.append((PROJ_AT[n], 2, None, "A"))
    steps += due
    if project and len(PAIR_EXPS) in PROJ_AT:
        steps.append((PROJ_AT[len(PAIR_EXPS)], 2, None, "A"))
    if maxes:
        steps += [("shift", h, None, "A") for h in range(2)]
    if exps:
        steps.append(("sums", 0, None, "A"))
    return steps


class Turn:

    def __init__(self, steps, times=1, after=None):
        self.steps, self.times = steps, times
        self.before = after
        self.n0 = after.n0 + after.times * len(after.steps) if after else 0
        self.c0 = {e: (after.c0[e] + after.times * after.reads(e)) if after else 0 for e in "AV"}
        assert times == 1 or len(steps) % RING == 0

    def reads(self, e, upto=None):
        return sum(s[-1] == e for s in self.steps[:upto])

    def filled(self, k, i):
        return self.n0 + k + 1 + i * len(self.steps)

    def read(self, e, k, i):
        return self.c0[e] + self.reads(e, k + 1) + i * self.reads(e)

    def bank(self, k):
        return 2 * ((self.n0 + k) % RING)

    def freed(self, k, i):
        if k >= RING:
            e = self.steps[k - RING][-1]
            return [(e, self.read(e, k - RING, i))]
        back = RING - k
        last = self.before
        if last is None:
            return []
        if self.times > 1 and [s[-1] for s in self.steps[-RING:]] != [s[-1] for s in last.steps[-RING:]]:
            return [(e, self.c0[e] + i * self.reads(e)) for e in "AV"] if k == 0 else []
        e = last.steps[-back][-1]
        later = sum(s[-1] == e for s in last.steps[len(last.steps) - back + 1 :])
        return [(e, self.c0[e] - later + i * self.reads(e))]


SETS = 3
GROUP_FIRST = Turn(
    [("k", 0, 0, "A"), ("k", 0, 1, "A"), ("q", 0, None, "V")]
    + [("max", 0, m, "V") for m in MAX_STEPS]
    + [("shifted_q", 0, None, "V"), ("k", 1, 0, "A"), ("k", 1, 1, "A"), ("q", 1, None, "V")]
)
GROUP_LOOP = Turn(SETS * group_steps(True, True, True), (G - 2) // SETS, GROUP_FIRST)
GROUP_LAST = Turn(group_steps(True, True, False) + group_steps(True, False, False), 1, GROUP_LOOP)
FIRST_MAXES = pair_steps(False, True, False)
PAIR_FIRST = Turn(
    [("proj_q", 1, None, "A"), ("proj_k", 1, None, "A"), ("proj_v", 1, None, "A")] + FIRST_MAXES[:-2]
    + [("proj_q", 2, None, "A"), ("proj_k", 2, None, "A"), ("proj_v", 2, None, "A")] + FIRST_MAXES[-2:],
    1, GROUP_LAST
)


def pair_turns():
    turns, after = [], PAIR_FIRST
    for b in range(B):
        loop = Turn(SETS * pair_steps(True, True, True), (NP - 2) // SETS, after)
        ends = b == B - 1
        last = Turn(pair_steps(True, True, not ends) + pair_steps(True, not ends, not ends)
                    + [("wo", 0, None, "V")], 1, loop)
        turns.append((loop, last))
        after = last
    return turns


PAIR_TURNS = pair_turns()


def macaron_block_kernel(nc, x, w_kqv, w_o0, w_int, w_scale, bias, w_q, w_k, w_v, w_o1, w_gate, w_up,
                         w_down, ident, mask_q, mask_k, head_mask, rope_cos, rope_sin, out):
    ctx = ExitStack()
    with ctx:
        def sb(name, shape, dt=F32):
            return ctx.enter_context(nc.sbuf_tensor(name, shape, dt))

        def sem(name):
            return ctx.enter_context(nc.semaphore(name))

        X = sb("X", [P, B, T, P])
        work = sb("work", [P, 2, B, T, P])
        D = work[:, 0]
        W = work[:, 1]
        XQ = sb("XQ", [P, B, T, P], BF16)
        XQT = sb("XQT", [P, B, S], BF16)
        XT = sb("XT", [P, B, S])
        ffn_h = sb("ffn_h", [P, HC, S])
        big = sb("big", [P, 16384])
        Pr = sb("Pr", [P, 2, GH, S])
        ffn_g = Pr[:, 0, 2:4, :]
        V0 = sb("V0", [P, G, T, GH * D0])
        vs_01 = sb("vs_01", [P, 2, T, GH, 32])
        OT = sb("OT", [P, S])
        acts = sb("acts", [P, G, T, GH * D0])
        stats = sb("stats", [P, 16, B, T])
        mx0 = sb("mx0", [P, T, GH])
        mr0 = sb("mr0", [P, 2, T, GH])
        rs0 = sb("rs0", [P, T, GH])
        mx1 = sb("mx1", [P, 2, T])
        sh1 = sb("sh1", [P, 2, T, 2], F16)
        wmax = sb("wmax", [P, 2])
        wsum = sb("wsum", [P, 2])
        qk_scale = sb("qk_scale", [P, 2])
        exp_scale = sb("exp_scale", [P, 1])
        wkqv_s = sb("wkqv_s", [P, 3 * P])
        wo0_s = sb("wo0_s", [P, P])
        wint_s = sb("wint_s", [P, P], BF16)
        wsc_s = sb("wsc_s", [P, P])
        bias_s = sb("bias_s", [P, P])
        wqkv1 = sb("wqkv1", [P, 3, H * D1])
        wo1_s = sb("wo1_s", [P, NP, P])
        wg_s = sb("wg_s", [P, 2, HID])
        wd_s = sb("wd_s", [P, HC, P])
        id_s = sb("id_s", [P, P])
        idb_s = sb("idb_s", [P, P], BF16)
        idh_s = sb("idh_s", [P, P], F16)
        ones_s = sb("ones_s", [P, P])
        mq_s = sb("mq_s", [P, P], BF16)
        mk_s = sb("mk_s", [P, P], BF16)
        hm_s = sb("hm_s", [P, 2])

        bigb = big[:, :].bitcast(BF16)
        Qs = bigb[:, 0:16384].rearrange("p (n t s c) -> p n t s c", n=B * NP, t=T, s=SLOTS)
        Ks = bigb[:, 16384:32768].rearrange("p (n t s c) -> p n t s c", n=B * NP, t=T, s=SLOTS)
        kt_01 = work[:, :, :, :, :].rearrange("p w b t c -> p (w b t c)").bitcast(BF16).rearrange(
            "p (r h s) -> p r h s", r=2, h=GH)
        kt_2 = XT[:, :, :].rearrange("p b s -> p (b s)").bitcast(BF16).rearrange("p (h s) -> p h s", h=GH)
        KT = [kt_01[:, 0], kt_01[:, 1], kt_2]
        QT = ffn_h[:, 0].bitcast(BF16).rearrange("p (n s) -> p n s", n=2)
        QmT = [a.rearrange("p (n s) -> p n s", n=2)
               for a in (ffn_h[:, 1].bitcast(BF16), ffn_h[:, 2].bitcast(BF16),
                         XQT[:, :, :].rearrange("p b s -> p (b s)"))]
        VS = [vs_01[:, 0], vs_01[:, 1], XQ[:, :, :, :].rearrange("p b t c -> p (b t c)").bitcast(F32).rearrange(
            "p (t h c) -> p t h c", t=T, h=GH)]
        qk_01 = big[:, 0:8192].bitcast(F16).rearrange("p (r m h s) -> p r m h s", r=2, m=4, h=2)
        qk_2 = work[:, :, :, :, :].rearrange("p w b t c -> p (w b t c)").bitcast(F16).rearrange(
            "p (m h s) -> p m h s", m=4, h=2)
        Q1, K1, Q2, K2 = ([qk_01[:, 0, m], qk_01[:, 1, m], qk_2[:, m]] for m in range(4))
        YT = big[:, 8192:16384].rearrange("p (n s) -> p n s", n=NP)
        by_head = lambda ap: ap.rearrange("p (h s) -> p h s", h=2)
        Psum = [Pr[:, 0, 0:2], Pr[:, 0, 2:4], by_head(acts[:, :, :, :].rearrange("p g t c -> p (g t c)"))]
        Pr1 = [Pr[:, 1, 0:2], Pr[:, 1, 2:4], by_head(vs_01[:, :, :, :, :].rearrange("p r t h c -> p (r t h c)"))]
        qk_raw = by_head(V0[:, :, :, :].rearrange("p g t c -> p (g t c)"))
        V1 = [ffn_h[:, r].rearrange("p (t c) -> p t c", t=T) for r in range(SETS)]
        y_raw = OT
        sums_s = XQ[:, :, :, :].rearrange("p b t c -> p (b t c)").bitcast(F32)
        rec_s = XQT[:, :, :].rearrange("p b s -> p (b s)").bitcast(F32)
        ws1 = sb("ws1", [P, SETS, 2, P])
        prf = Pr[:, :, :, :].rearrange("p r h s -> p (r h s)")
        cosT = prf[:, 0:2048].rearrange("p (t c) -> p t c", t=T)
        sinT = prf[:, 2048:4096].rearrange("p (t c) -> p t c", t=T)
        R = prf[:, 4096:5120].rearrange("p (t c) -> p t c", t=4)
        R2 = prf[:, 5120:6144].rearrange("p (t c) -> p t c", t=4)
        raw_gu = ffn_h[:, 0, 0:2 * HID].bitcast(I32).rearrange("p (a c) -> p a c", a=2)
        raw_masks = ffn_h[:, 2, 2 * P:4 * P].rearrange("p (a c) -> p a c", a=2)
        raw_int = ffn_h[:, 2, 0:2 * P].bitcast(I64)
        raw_d = ffn_h[:, 1, 0:HID].bitcast(I32).rearrange("p (a c) -> p a c", a=HC)

        ps = ctx.enter_context(nc.psum_tensor("ps", [P, 8, 512], F32))

        def banks(b, n):
            return ps[:, b:b + n, :].rearrange("p a c -> p (a c)")

        def ubank(key):
            return 4 * (UNIT_AT[key] % 2)

        x_in = [sem(f"x_in_{b}") for b in range(B)]
        w_in, k_in = sem("w_in"), sem("k_in")
        wprep = sem("wprep")
        centred, squared, var_ready, sd_ready = sem("centred"), sem("squared"), sem("var_ready"), sem("sd_ready")
        norm_ready = sem("norm_ready")
        pe_unit, act_unit, dve_unit = sem("pe_unit"), sem("act_unit"), sem("dve_unit")
        split_done, dups_done, slots_set = sem("split_done"), sem("dups_done"), sem("slots_set")
        ring_filled, ring_act, ring_dve = sem("ring_filled"), sem("ring_act"), sem("ring_dve")
        ring_read = {"A": ring_act, "V": ring_dve}
        shift_ready, acts_laid = sem("shift_ready"), sem("acts_laid")
        v_staged, vs_set = sem("v_staged"), sem("vs_set")
        pv0, acc0_saved = sem("pv0"), sem("acc0_saved")
        pv1, acc1_saved = sem("pv1"), sem("acc1_saved")
        rows_set, w_staged = sem("rows_set"), sem("w_staged")
        wmax_ready, scale_ready, w_scaled = sem("wmax_ready"), sem("scale_ready"), sem("w_scaled")
        high_done, low_done, copy_done = sem("high_done"), sem("low_done"), sem("copy_done")
        shift1_ready = sem("shift1_ready")
        summed = sem("summed")
        y_done = sem("y_done")
        dve_step = sem("dve_step")
        pe_gate = sem("pe_gate")
        out_done = sem("out_done")

        block = ctx.enter_context(nc.Block())
        x_v = x.rearrange("(b t p) c -> p b t c", b=B, t=T)
        o_v = out.rearrange("(b t p) c -> p b t c", b=B, t=T)

        @block.sync
        def _(sp):
            for b in range(B):
                sp.dma_start(X[:, b], x_v[:, b]).then_inc(x_in[b], 16)
            sp.dma_start(wkqv_s[:], w_kqv).then_inc(w_in, 16)
            sp.dma_start(cosT, rope_cos).then_inc(w_in, 16)
            sp.dma_start(sinT, rope_sin).then_inc(w_in, 16)
            sp.dma_start(raw_gu[:, 0, :], w_gate).then_inc(w_in, 16)
            sp.dma_start(raw_gu[:, 1, :], w_up).then_inc(w_in, 16)
            sp.dma_start(raw_d, w_down.rearrange("(n p) c -> p n c", p=P)).then_inc(w_in, 16)
            sp.dma_start(wo0_s[:], w_o0).then_inc(w_in, 16)
            for n, w in enumerate((w_q, w_k, w_v)):
                sp.dma_start(wqkv1[:, n, :], w).then_inc(w_in, 16)
            sp.dma_start(wo1_s[:], w_o1.rearrange("(n p) c -> p n c", p=P)).then_inc(w_in, 16)
            for b in range(B):
                sp.wait_ge(dve_unit, read_by("V", UNIT_AT[("mm", 5, b)]))
                sp.dma_start(o_v[:, b], X[:, b]).then_inc(out_done, 16)
            sp.wait_ge(out_done, 16 * B)

        K_LOADS, W_LOADS = 7, 11
        EARLY = (4, 5)
        FREE = 2
        START = 1

        @block.gpsimd
        def _(pool):
            g = nc.gpsimd
            g.memset(Qs[:, :, :, 6:8, :].rearrange("p n t s c -> p (n t) (s c)"), 0.0)
            g.memset(Ks[:, :, :, 6:8, :].rearrange("p n t s c -> p (n t) (s c)"), 0.0).then_inc(slots_set, 1)
            g.memset(vs_01[:], 0.0).then_inc(vs_set, 1)
            pool.wait_ge(slots_set, 1)
            g.memset(Ks[:, :, :, SHIFT_SLOT, :].rearrange("p n t (h d) -> p (n t) h d", h=2)[:, :, :, 0:3],
                     1.0).then_inc(slots_set, 1)
            pool.wait_ge(pe_unit, filled(("turn", 0, B - 1)))
            g.memset(VS[2], 0.0).then_inc(vs_set, 1)
            pool.wait_ge(vs_set, 2)
            for r in range(SETS):
                g.memset(VS[r][:, :, :, D0:D0 + 1].rearrange("p t h c -> p (t h) c"), 1.0).then_inc(vs_set, 1)

            pool.wait_ge(vs_set, 2 + SETS)
            pool.wait_ge(act_unit, read_by("A", UNIT_AT[("qkv", B - 1, 1)]))
            for group in range(G):
                if group >= SETS:
                    pool.wait_ge(pv0, T * (group - SETS + 1) + FREE)
                g.tensor_copy(VS[group % SETS][:, :, :, 0:D0],
                              V0[:, group].rearrange("p t (h d) -> p t h d", h=GH)).then_inc(v_staged, 1)

            pool.wait_ge(ring_filled, GROUP_LAST.filled(len(GROUP_LAST.steps) - 1, 0))
            for r in range(SETS):
                if r == SETS - 1:
                    pool.wait_ge(pe_unit, filled(("turn", 4, B - 1)))
                g.memset(Q2[r][D1:P], 0.0)
                g.memset(K2[r][D1:P], 0.0).then_inc(rows_set, 1)
                pool.wait_ge(rows_set, 3 * r + 1)
                g.memset(K2[r][D1:D1 + 2], SHIFT_LOW).then_inc(rows_set, 1)
                pool.wait_ge(rows_set, 3 * r + 2)
                g.memset(K2[r][D1:D1 + 1], SHIFT_TOP).then_inc(rows_set, 1)
                pool.wait_ge(rows_set, 3 * r + 3)
            def stage_weights(n, r):
                g.tensor_copy(ws1[:, r], wqkv1[:, 0:2, bass.ds(n * P, P)]).then_inc(w_staged, 1)

            def low_parts(first, start):
                r, pair = first % SETS, first + start
                pool.wait_ge(high_done, 2 * pair + 2)
                for n, (low, high) in enumerate(((K1[r][D1:P], K1[r]), (Q2[r][0:D1], Q1[r]))):
                    for head in range(2):
                        rows = slice(head * D1, (head + 1) * D1)
                        if n or head or first:
                            pool.wait_ge(low_done, 4 * pair + 2 * n + head)
                        if not n and head:
                            pool.wait_ge(copy_done, 2 * pair + 2)
                        g.tensor_tensor(low[:, head], qk_raw[rows, 1 - n], high[rows, head],
                                        ALU.subtract).then_inc(low_done, 1)

            def pair_turn(turn, i, first, start):
                done = 0
                for k, (kind, h, arg, reader) in enumerate(turn.steps):
                    pair = first + start + done
                    if kind == "exp":
                        t, j, n = arg
                        if (t, j) == (0, 0) and first + done + 2 < B * NP:
                            pool.wait_ge(low_done, 4 * (pair + 2))
                            stage_weights((first + done + 2) % NP + start, (first + done + 2) % SETS)
                            pool.wait_ge(w_staged, pair + 3)
                        elif (t, j) == (0, 0):
                            pool.wait_ge(low_done, 4 * B * NP)
                        if t and j + n == 2:
                            pool.wait_ge(ring_act, turn.read("A", k, i))
                            pool.wait_ge(summed, (T - 1) * pair + t - 1 + START)
                            total = Psum[(first + done) % SETS][:, :, t * P:]
                            g.tensor_tensor(total, total, Pr1[(t - 1) % 3][:, :, 0:(T - t) * P], ALU.add).then_inc(summed, 1)
                    if turn is PAIR_FIRST and kind == "proj_v":
                        low_parts(first + h, 0)
                    if kind == "sums" and first + done + 2 < B * NP:
                        pool.wait_ge(summed, (T - 1) * (pair + 1) + START)
                        low_parts(first + done + 2, start)
                    if kind == "sums":
                        done += 1

            pool.wait_ge(w_scaled, 1)
            pool.wait_ge(rows_set, 3 * SETS)
            stage_weights(0, 0)
            stage_weights(1, 1)
            pool.wait_ge(w_staged, 2)
            pair_turn(PAIR_FIRST, 0, -1, 0)
            for b, (loop, last) in enumerate(PAIR_TURNS):
                with pool.Fori(0, loop.times) as i:
                    pair_turn(loop, i, b * NP, SETS * i)
                pair_turn(last, 0, (b + 1) * NP - 2, 0)

        @block.scalar
        def _(act):
            a = nc.scalar
            for dst, src in ((id_s[:], ident), (raw_int, w_int), (wsc_s[:], w_scale), (bias_s[:], bias),
                             (raw_masks[:, 0], mask_q), (raw_masks[:, 1], mask_k), (hm_s[:], head_mask)):
                act.dma_start(dst, src).then_inc(k_in, 16)

            def unit(key):
                act.wait_ge(pe_unit, filled(key))

            def ln_square(s, b):
                act.wait_ge(centred, B * s + b + 1)
                a.activation(W[:, b], D[:, b], ACT.Square).then_inc(squared, 1)

            def ln_root(s, b):
                act.wait_ge(var_ready, B * s + b + 1)
                a.activation(stats[:, 3, b, :], stats[:, 2, b, :], ACT.Sqrt).then_inc(sd_ready, 1)

            def turned(s, b, dst, bf=False):
                key = ("turn", s, b)
                unit(key)
                src = banks(ubank(key), 1).bitcast(BF16) if bf else banks(ubank(key), 2)
                a.activation(dst, src, ACT.Copy).then_inc(act_unit, 1)

            def norm(s):
                halves = range(int(s in EARLY), B)
                for b in halves:
                    ln_square(s, b)
                for b in halves:
                    ln_root(s, b)

            def gated(s):
                norm(s)
                for kind, b, c in GATED:
                    if kind == "turn":
                        turned(s, b, XT[:, b])
                    if kind == "up":
                        key = ("up", s, b, c)
                        unit(key)
                        last = ("up", s, b, c - 2) if c >= 2 else ("up", s, b - 1, c + 1) if b else None
                        if last:
                            act.wait_ge(dve_unit, read_by("V", UNIT_AT[last]))
                        a.activation(ffn_g[:, (HC * b + c) % 2], banks(ubank(key), 2), ACT.Silu).then_inc(act_unit, 1)
                    if kind == "mm" and s + 1 in EARLY and b == 0:
                        ln_square(s + 1, 0)
                        ln_root(s + 1, 0)

            norm(0)
            for b in range(B):
                turned(0, b, XQT[:, b], True)
            norm(1)
            for b in range(B):
                turned(1, b, XT[:, b])

            def copy_values(b, half):
                key = ("qkv", b, half)
                unit(key)
                src = ps[:, ubank(key):ubank(key) + 4, 2 * P:3 * P]
                a.activation(V0[:, b * GB:(b + 1) * GB, 4 * half:4 * half + 4, :].rearrange("p g t c -> p t g c"),
                             src.rearrange("p t (g c) -> p t g c", g=GB), ACT.Copy).then_inc(act_unit, 1)

            def copy_parts(b, half):
                act.wait_ge(split_done, 2 * b + half + 1)
                for stack, parts in ((Qs, Q_PARTS), (Ks, K_PARTS)):
                    for slot, part in enumerate(parts):
                        if slot != parts.index(part):
                            view = stack[:, b * NP:(b + 1) * NP, 4 * half:4 * half + 4]
                            ins = a.activation(view[:, :, :, slot, :], view[:, :, :, parts.index(part), :],
                                               ACT.Copy)
                ins.then_inc(dups_done, 1)

            halves = [(b, half) for b in range(B) for half in range(2)]
            for n, at in enumerate(halves):
                copy_values(*at)
                if n:
                    copy_parts(*halves[n - 1])
            copy_parts(*halves[-1])

            def group_turn(turn, i, g0):
                base, par = g0
                done = 0
                for k, (kind, ahead, arg, reader) in enumerate(turn.steps):
                    if kind == "heads":
                        done += 1
                        continue
                    if reader != "A":
                        continue
                    slot = banks(turn.bank(k), 2)
                    r = (par + done + ahead) % SETS
                    if kind == "k":
                        act.wait_ge(ring_filled, turn.filled(k, i))
                        for hh in range(2):
                            ins = a.activation(KT[r][:, 2 * arg + hh], slot.bitcast(BF16)[:, 0:S], ACT.Copy,
                                               scale=hm_s[:, hh:hh + 1])
                        ins.then_inc(ring_act, 1)
                    if kind == "exp":
                        t, j, n = arg
                        w = (T - t) * P
                        if j == 0:
                            act.wait_ge(pv0, T * (base + done) + t + 1)
                        act.wait_ge(ring_filled, turn.filled(k, i))
                        src = slot.rearrange("p (n c) -> p n c", n=n)[:, :, 0:w]
                        a.activation(Pr[:, t % 2, j:j + n, 0:w], src, ACT.Exp, scale=SCALE0).then_inc(ring_act, 1)
                        if t == T - 1:
                            act.wait_ge(pv0, T * (base + done + 1) + FREE)
                            a.activation(OT[:], banks(6, 2), ACT.Copy).then_inc(acc0_saved, 1)

            act.wait_ge(k_in, 16 * K_LOADS)
            group_turn(GROUP_FIRST, 0, (0, 0))
            with act.Fori(0, GROUP_LOOP.times) as i:
                group_turn(GROUP_LOOP, i, (SETS * i, 0))
            group_turn(GROUP_LAST, 0, (G - 2, 0))

            act.wait_ge(ring_dve, GROUP_LAST.read("V", len(GROUP_LAST.steps) - 1, 0))
            for b in range(B):
                a.activation(D[:, b].rearrange("p t (g c) -> p t g c", g=GB),
                             acts[:, b * GB:(b + 1) * GB].rearrange("p g t c -> p t g c"), ACT.Copy).then_inc(acts_laid, 1)
            for b in range(B):
                key = ("acts", b)
                unit(key)
                a.activation(XT[:, b], banks(ubank(key), 2), ACT.Copy).then_inc(act_unit, 1)
            act.wait_ge(scale_ready, 1)
            a.activation(wqkv1[:, 0], wqkv1[:, 0], ACT.Copy, scale=qk_scale[:, 0:1])
            a.activation(wqkv1[:, 1], wqkv1[:, 1], ACT.Copy, scale=qk_scale[:, 1:2]).then_inc(w_scaled, 1)
            norm(2)
            for b in range(B):
                turned(2, b, XQT[:, b], True)
            gated(3)
            norm(4)
            for b in range(B):
                turned(4, b, XT[:, b])

            def pair_turn(turn, i, first, start):
                done = 0
                for k, (kind, h, arg, reader) in enumerate(turn.steps):
                    slot = banks(turn.bank(k), 2)
                    if kind in ("proj_q", "proj_k"):
                        n, pair = int(kind == "proj_k"), first + start + done + h
                        if first + done + h > 0:
                            act.wait_ge(low_done, 4 * pair - 2 * n)
                        act.wait_ge(ring_filled, turn.filled(k, i))
                        a.activation(qk_raw[:, n], slot, ACT.Copy).then_inc(ring_act, 1)
                    if kind == "proj_v":
                        act.wait_ge(ring_filled, turn.filled(k, i))
                        a.activation(V1[(first + done + h) % SETS], slot.rearrange("p (t c) -> p t c", t=T),
                                     ACT.Copy).then_inc(ring_act, 1)
                    if kind == "shift":
                        act.wait_ge(ring_filled, turn.filled(k, i))
                        a.activation(Q2[(first + done + 1) % SETS][D1:D1 + 2, h],
                                     slot.bitcast(F16)[D1:D1 + 2, 0:S], ACT.Copy).then_inc(ring_act, 1)
                    if kind == "exp":
                        t, j, n = arg
                        w, pair = (T - t) * P, first + start + done
                        if j == 0 and (t == 1 or t > 3):
                            behind = max(t - 3, 0)
                            act.wait_ge(pv1, T * pair + behind + (t > 1) + START)
                            act.wait_ge(summed, (T - 1) * pair + behind + START)
                        act.wait_ge(ring_filled, turn.filled(k, i))
                        dst = Pr1[(t - 1) % 3] if t else Psum[(first + done) % SETS]
                        a.activation(dst[:, j:j + n, 0:w], slot.rearrange("p (n c) -> p n c", n=n)[:, :, 0:w],
                                     ACT.Exp, scale=exp_scale[:, 0:1]).then_inc(ring_act, 1)
                        if turn is PAIR_TURNS[-1][1] and done == 1 and j + n == 2 and t in (3, 5):
                            (ln_square if t == 3 else ln_root)(5, 0)
                        if t == T - 1:
                            act.wait_ge(pv1, T * (pair + 1) + START)
                            act.wait_ge(y_done, pair + START)
                            a.activation(y_raw[:], banks(6, 2), ACT.Copy).then_inc(acc1_saved, 1)
                    if kind == "sums":
                        act.wait_ge(ring_filled, turn.filled(k, i))
                        a.activation(sums_s, slot, ACT.Copy).then_inc(ring_act, 1)
                        done += 1

            pair_turn(PAIR_FIRST, 0, -1, 0)
            for b, (loop, last) in enumerate(PAIR_TURNS):
                with act.Fori(0, loop.times) as i:
                    pair_turn(loop, i, b * NP, SETS * i)
                pair_turn(last, 0, (b + 1) * NP - 2, 0)
            gated(5)

        @block.vector
        def _(dve):
            v = nc.vector
            steps = [0, None, 0]

            def link(ins):
                ins.then_inc(dve_step, 1)
                steps[0] += 1
                dve.wait_ge(dve_step, steps[0] if steps[1] is None else steps[0] + steps[1] * steps[2])

            def small(ap):
                return ap.unsqueeze(2).to_broadcast([P, T, P])

            v.memset(ones_s[:], 1.0)
            v.sem_inc(pv0, FREE)
            for counted in (pv1, summed, acc0_saved, acc1_saved, y_done):
                v.sem_inc(counted, START)

            def centre(s, b):
                if s == 0:
                    dve.wait_ge(x_in[b], 16)
                link(v.reduce_sum(stats[:, 0, b, :], X[:, b], AX.X))
                link(v.tensor_scalar(stats[:, 1, b, :], stats[:, 0, b, :], 1.0 / P, None, ALU.mult))
                v.tensor_tensor(D[:, b], X[:, b], small(stats[:, 1, b, :]), ALU.subtract).then_inc(centred, 1)

            def variance(s, b):
                dve.wait_ge(squared, B * s + b + 1)
                link(v.reduce_sum(stats[:, 0, b, :], W[:, b], AX.X))
                v.tensor_scalar(stats[:, 2, b, :], stats[:, 0, b, :], 1.0 / P, LN_EPS, ALU.mult,
                                ALU.add).then_inc(var_ready, 1)

            def normalise(s, b):
                dve.wait_ge(sd_ready, B * s + b + 1)
                r, t, var = stats[:, 4, b, :], stats[:, 5, b, :], stats[:, 2, b, :]
                link(v.reciprocal(r, stats[:, 3, b, :]))
                link(v.tensor_tensor(t, r, r, ALU.mult))
                link(v.tensor_tensor(t, t, var, ALU.mult))
                link(v.tensor_scalar(t, t, -0.5, 1.5, ALU.mult, ALU.add))
                link(v.tensor_tensor(r, r, t, ALU.mult))
                return v.tensor_tensor(D[:, b], D[:, b], small(r), ALU.mult)

            def norm(s, to_turn=True):
                halves = range(int(s in EARLY), B)
                for b in halves:
                    centre(s, b)
                for b in halves:
                    variance(s, b)
                for b in halves:
                    ins = normalise(s, b)
                    if to_turn:
                        ins.then_inc(norm_ready, 1)
                    else:
                        link(ins)

            def prepare():
                dve.wait_ge(k_in, 16 * K_LOADS)
                v.tensor_copy(idb_s[:], id_s[:])
                v.tensor_copy(idh_s[:], id_s[:])
                v.tensor_copy(mq_s[:], raw_masks[:, 0])
                v.tensor_copy(mk_s[:], raw_masks[:, 1])
                v.tensor_copy(wint_s[:], raw_int.bitcast(I32).rearrange("p (c two) -> p c two", two=2)[:, :, 0]).then_inc(wprep, 1)
                v.tensor_scalar(wsc_s[:], wsc_s[:], 0.5, None, ALU.mult)
                link(v.tensor_scalar(bias_s[:], bias_s[:], 0.5, None, ALU.mult))

            def int_ffn(s):
                norm(s, False)
                if s == 0:
                    prepare()
                for b in range(B):
                    amax, xs, inv = stats[:, 6, b, :], stats[:, 7, b, :], stats[:, 8, b, :]
                    link(v.tensor_reduce(amax, D[:, b], AX.X, ALU.max, apply_absolute_value=True))
                    link(v.tensor_scalar(xs, amax, Q_EPS, 1.0 / 127.0, ALU.max, ALU.mult))
                    link(v.reciprocal(inv, xs))
                    link(v.tensor_tensor(W[:, b], D[:, b], small(inv), ALU.mult))
                    link(v.tensor_scalar(W[:, b], W[:, b], MAGIC, MAGIC, ALU.add, ALU.subtract))
                    v.tensor_scalar(XQ[:, b], W[:, b], 127.0, -128.0, ALU.min, ALU.max).then_inc(norm_ready, 1)
                for b in range(B):
                    key = ("mm", s, b)
                    dve.wait_ge(pe_unit, filled(key))
                    acc = banks(ubank(key), 2).rearrange("p (t c) -> p t c", t=T)
                    for t in range(T):
                        ins = v.scalar_tensor_tensor(W[:, b, t], acc[:, t], stats[:, 7, b, t:t + 1], wsc_s[:],
                                                     ALU.mult, ALU.mult)
                    ins.then_inc(dve_unit, 1)
                    dve.wait_ge(dve_unit, read_by("V", UNIT_AT[key]))
                    link(v.tensor_tensor(W[:, b], W[:, b], bias_s[:].unsqueeze(1).to_broadcast([P, T, P]), ALU.add))
                    link(v.tensor_tensor(X[:, b], X[:, b], W[:, b], ALU.add))

            def add_to_x(key, b, factor):
                dve.wait_ge(pe_unit, filled(key))
                acc = banks(ubank(key), 2).rearrange("p (t c) -> p t c", t=T)
                v.scalar_tensor_tensor(X[:, b], acc, factor, X[:, b], ALU.mult, ALU.add).then_inc(dve_unit, 1)
                dve.wait_ge(dve_unit, read_by("V", UNIT_AT[key]))

            def gated(s):
                norm(s)
                for kind, b, c in GATED:
                    if kind == "up":
                        key = ("up", s, b, c)
                        if (b, c) == (1, 0):
                            dve.wait_ge(pe_unit, filled(("mm", s, 0)))
                        dve.wait_ge(act_unit, read_by("A", UNIT_AT[key]))
                        dve.wait_ge(pe_unit, filled(key))
                        v.tensor_tensor(ffn_h[:, c], ffn_g[:, (HC * b + c) % 2], banks(ubank(key) + 2, 2),
                                        ALU.mult).then_inc(dve_unit, 1)
                    if kind == "mm":
                        add_to_x(("mm", s, b), b, 0.5)
                        if s + 1 in EARLY and b == 0:
                            centre(s + 1, 0)
                            variance(s + 1, 0)
                            normalise(s + 1, 0).then_inc(norm_ready, 1)

            int_ffn(0)

            norm(1)
            dve.wait_ge(w_in, 16 * W_LOADS)
            for b in range(B):
                for half in range(2):
                    key = ("qkv", b, half)
                    dve.wait_ge(pe_unit, filled(key))
                    dve.wait_ge(act_unit, read_by("A", UNIT_AT[key]))
                    t0 = 4 * half
                    kq = ps[:, ubank(key):ubank(key) + 4, 0:2 * P]
                    pairs = kq.rearrange("p t (n two) -> p t n two", two=2)
                    sp = sinT[:, t0:t0 + 4].rearrange("p t (n two) -> p t n two", two=2)
                    r2 = R2.rearrange("p t (n two) -> p t n two", two=2)
                    if (b, half) != (0, 0):
                        dve.wait_ge(split_done, 2 * b + half)
                    v.tensor_tensor(R, kq, cosT[:, t0:t0 + 4], ALU.mult)
                    v.tensor_tensor(r2[:, :, :, 0], pairs[:, :, :, 1], sp[:, :, :, 0], ALU.mult)
                    v.tensor_tensor(r2[:, :, :, 1], pairs[:, :, :, 0], sp[:, :, :, 1], ALU.mult).then_inc(dve_unit, 1)
                    dve.wait_ge(dve_unit, read_by("V", UNIT_AT[key]))
                    link(v.tensor_tensor(R, R, R2, ALU.add))
                    for n, (stack, parts) in enumerate(((Ks, K_PARTS), (Qs, Q_PARTS))):
                        rest = R[:, :, n * P:(n + 1) * P].rearrange("p t (n c) -> p t n c", n=NP)
                        view = stack[:, b * NP:(b + 1) * NP, t0:t0 + 4]
                        for part in range(3):
                            dst = view[:, :, :, parts.index(part), :].rearrange("p n t c -> p t n c")
                            ins = v.tensor_copy(dst, rest)
                            if part < 2:
                                link(ins)
                                link(v.tensor_tensor(rest, rest, dst, ALU.subtract))
                    ins.then_inc(split_done, 1)

            v.tensor_scalar(wg_s[:], raw_gu, W_SCALE, None, ALU.mult)
            v.tensor_scalar(wd_s[:], raw_d, W_SCALE, None, ALU.mult).then_inc(wprep, 1)
            dve.wait_ge(wprep, 2)

            def group_turn(turn, i, base, next_group, par=0):
                done = 0
                for k, (kind, ahead, arg, reader) in enumerate(turn.steps):
                    if reader != "V":
                        continue
                    dve.wait_ge(ring_filled, turn.filled(k, i))
                    slot = banks(turn.bank(k), 2)
                    if kind == "max":
                        t, j, n = arg
                        src = slot.rearrange("p (n c) -> p n c", n=n)[:, :, 0:(t + 1) * P]
                        v.tensor_reduce(mx0[:, t, j:j + n], src, AX.X, ALU.max, negate=True).then_inc(ring_dve, 1)
                        if (t, j + n) == (T - 1, GH):
                            dve.wait_ge(ring_dve, turn.read("V", k, i))
                            view = Qs[:, bass.ds(2 * (next_group + done), 2), :, SHIFT_SLOT, :]
                            view = view.rearrange("p a t (h d) -> p a t h d", h=2)
                            by_pair = [m.rearrange("p t (a h) -> p a t h", a=2) for m in (mx0[:], mr0[:, 0], mr0[:, 1])]
                            link(v.tensor_copy(view[:, :, :, :, 0], by_pair[0]))
                            link(v.tensor_tensor(by_pair[1], by_pair[0], view[:, :, :, :, 0], ALU.subtract))
                            link(v.tensor_copy(view[:, :, :, :, 1], by_pair[1]))
                            link(v.tensor_tensor(by_pair[2], by_pair[1], view[:, :, :, :, 1], ALU.subtract))
                            v.tensor_copy(view[:, :, :, :, 2], by_pair[2]).then_inc(shift_ready, 1)
                    if kind in ("q", "shifted_q"):
                        dst = QT if kind == "q" else QmT[(par + done + ahead) % SETS]
                        v.tensor_copy(dst, slot.bitcast(BF16).rearrange("p (n s) -> p n s", n=2)).then_inc(ring_dve, 1)
                    if kind == "heads":
                        src = slot.rearrange("p (t h c) -> p t h c", t=T, h=GH)
                        link(v.reciprocal(rs0[:], src[:, :, :, D0]))
                        v.tensor_tensor(acts[:, base + done].rearrange("p t (h d) -> p t h d", h=GH),
                                        src[:, :, :, 0:D0], rs0[:].unsqueeze(3).to_broadcast([P, T, GH, D0]),
                                        ALU.mult).then_inc(ring_dve, 1)
                        done += 1

            def looped(times, links, body):
                start = steps[0]
                with dve.Fori(0, times) as i:
                    steps[1:] = [i, links]
                    body(i)
                assert steps[0] == start + links, (steps[0] - start, links)
                steps[:] = [start + links * times, None, 0]

            group_turn(GROUP_FIRST, 0, 0, 0)
            looped(GROUP_LOOP.times, 5 * SETS, lambda i: group_turn(GROUP_LOOP, i, SETS * i, SETS * i + 1))
            group_turn(GROUP_LAST, 0, G - 2, G - 1)
            v.tensor_reduce(wmax[:, 0:1], wqkv1[:, 0], AX.X, ALU.max, apply_absolute_value=True)
            v.tensor_reduce(wmax[:, 1:2], wqkv1[:, 1], AX.X, ALU.max,
                            apply_absolute_value=True).then_inc(wmax_ready, 1)
            dve.wait_ge(pe_unit, filled(("wscale",)))
            v.tensor_scalar(wsum[:], ps[:, ubank(("wscale",)), 0:2], 1e-15, None, ALU.max).then_inc(dve_unit, 1)
            dve.wait_ge(dve_unit, read_by("V", UNIT_AT[("wscale",)]))
            link(v.reciprocal(wsum[:], wsum[:]))
            link(v.tensor_scalar(wsum[:], wsum[:], QK_BOUND / float(P) ** 0.5, None, ALU.mult))
            link(v.tensor_scalar(qk_scale[:].bitcast(I32), wsum[:].bitcast(I32), 0x7F800000, None,
                                 ALU.bitwise_and))
            link(v.tensor_tensor(exp_scale[:], qk_scale[:, 0:1], qk_scale[:, 1:2], ALU.mult))
            link(v.reciprocal(exp_scale[:], exp_scale[:]))
            link(v.tensor_scalar(exp_scale[:], exp_scale[:], SCALE1, None, ALU.mult))
            v.sem_inc(scale_ready, 1)
            for b in range(B):
                add_to_x(("mm", 1, b), b, 1.0)
            int_ffn(2)
            gated(3)
            norm(4)

            def pair_turn(turn, i, first, start):
                done = 0
                for k, (kind, h, arg, reader) in enumerate(turn.steps):
                    slot = banks(turn.bank(k), 2)
                    if kind in ("proj_q", "proj_k"):
                        n = 2 * (first + start + done + h) + (2 if kind == "proj_k" else 1)
                        r = (first + done + h) % SETS
                        dve.wait_ge(ring_act, turn.read("A", k, i))
                        stack, raw = (Q1[r], qk_raw[:, 0]) if kind == "proj_q" else (K1[r], qk_raw[:, 1])
                        v.tensor_copy(stack[0:D1, 0], raw[0:D1])
                        v.tensor_copy(stack[D1:P, 1], raw[D1:P]).then_inc(high_done, 1)
                        dve.wait_ge(high_done, n)
                        if kind == "proj_q":
                            v.tensor_copy(stack[D1:P, 0], stack[0:D1, 0])
                        else:
                            v.tensor_copy(K2[r][0:D1, 0], stack[0:D1, 0])
                            v.tensor_copy(K2[r][0:D1, 1], stack[D1:P, 1])
                        v.tensor_copy(stack[0:D1, 1], stack[D1:P, 1]).then_inc(copy_done, 1)
                    if kind == "max":
                        t, j, n = arg
                        dve.wait_ge(ring_filled, turn.filled(k, i))
                        src = slot.rearrange("p (n c) -> p n c", n=n)[:, :, 0:(t + 1) * P]
                        v.tensor_reduce(mx1[:, j:j + n, t], src, AX.X, ALU.max, negate=True).then_inc(ring_dve, 1)
                        if (t, j + n) == (T - 1, 2):
                            dve.wait_ge(ring_dve, turn.read("V", k, i))
                            link(v.tensor_scalar(mx1[:], mx1[:], 1 / SHIFT_TOP, None, ALU.mult))
                            link(v.tensor_copy(sh1[:, :, :, 0], mx1[:]))
                            link(v.tensor_tensor(mx1[:], mx1[:], sh1[:, :, :, 0], ALU.subtract))
                            v.tensor_scalar(sh1[:, :, :, 1], mx1[:], SHIFT_TOP / SHIFT_LOW, None,
                                            ALU.mult).then_inc(shift1_ready, 1)
                    if kind == "sums":
                        dve.wait_ge(ring_act, turn.read("A", k, i))
                        link(v.reciprocal(rec_s, sums_s))
                        v.tensor_tensor(YT[:, bass.ds((first + done) % NP + start, 1)].rearrange("p n s -> p (n s)"),
                                        y_raw[:], rec_s, ALU.mult).then_inc(y_done, 1)
                        done += 1
                        if turn is PAIR_TURNS[-1][1] and done == 1:
                            dve.wait_ge(ring_filled, turn.filled(k, i))
                            centre(5, 0)
                            variance(5, 0)
                            normalise(5, 0).then_inc(norm_ready, 1)
                    if kind == "wo":
                        dve.wait_ge(ring_filled, turn.filled(k, i))
                        half = X[:, first // NP]
                        v.tensor_tensor(half, slot.rearrange("p (t c) -> p t c", t=T), half,
                                        ALU.add).then_inc(ring_dve, 1)

            pair_turn(PAIR_FIRST, 0, -1, 0)
            for b, (loop, last) in enumerate(PAIR_TURNS):
                looped(loop.times, 4 * SETS, lambda i: pair_turn(loop, i, b * NP, SETS * i))
                pair_turn(last, 0, (b + 1) * NP - 2, 0)
            dve.wait_ge(ring_dve, last.read("V", len(last.steps) - 1, 0))
            gated(5)

        @block.tensor
        def _(pe):
            te = nc.tensor

            def unit(key, ring=None):
                n = UNIT_AT[key]
                if n >= 2:
                    for e, s in (("A", act_unit), ("V", dve_unit)):
                        if e in UNITS[n - 2][1]:
                            pe.wait_ge(s, read_by(e, n - 2))
                if ring:
                    for e in "AV":
                        pe.wait_ge(ring_read[e], ring.read(e, len(ring.steps) - 1, 0))
                return ubank(key)

            def turn_half(key, src, ident_ap, bf=False, ring=None):
                b0 = unit(key, ring)
                for t in range(T):
                    if bf:
                        dst = banks(b0, 1).bitcast(BF16)[:, t * P:(t + 1) * P]
                    else:
                        dst = banks(b0, 2)[:, t * P:(t + 1) * P]
                    ins = te.transpose(dst, src(t), ident_ap)
                ins.then_inc(pe_unit, 1)

            def int_ffn(s):
                for b in range(B):
                    pe.wait_ge(norm_ready, B * s + b + 1)
                    turn_half(("turn", s, b), lambda t: XQ[:, b, t], idb_s[:], True)
                    key = ("mm", s, b)
                    b0 = unit(key)
                    pe.wait_ge(act_unit, read_by("A", UNIT_AT[("turn", s, b)]))
                    for t in range(T):
                        ins = te.matmul(banks(b0, 2)[:, t * P:(t + 1) * P], XQT[:, b, t * P:(t + 1) * P],
                                        wint_s[:], start=True, stop=True)
                    ins.then_inc(pe_unit, 1)

            def gated(s):
                for kind, b, c in GATED:
                    if kind == "turn":
                        pe.wait_ge(norm_ready, B * s + b + 1)
                        turn_half(("turn", s, b), lambda t: D[:, b, t], id_s[:],
                                  ring=PAIR_TURNS[-1][1] if (s, b) == (5, 0) else None)
                    if kind == "up":
                        key = ("up", s, b, c)
                        b0 = unit(key)
                        pe.wait_ge(act_unit, read_by("A", UNIT_AT[("turn", s, b)]))
                        for m in range(2):
                            for n in range(2):
                                ins = te.matmul(ps[:, b0 + 2 * m + n], wg_s[:, m, c * P:(c + 1) * P],
                                                XT[:, b, 512 * n:512 * n + 512], start=True, stop=True)
                        ins.then_inc(pe_unit, 1)
                    if kind == "mm":
                        key = ("mm", s, b)
                        b0 = unit(key)
                        pe.wait_ge(dve_unit, read_by("V", UNIT_AT[("up", s, b, HC - 1)]))
                        for t in range(T):
                            for h in range(HC):
                                ins = te.matmul(banks(b0, 2)[:, t * P:(t + 1) * P], ffn_h[:, h, t * P:(t + 1) * P],
                                                wd_s[:, h], start=h == 0, stop=h == HC - 1)
                        ins.then_inc(pe_unit, 1)

            pe.wait_ge(k_in, 16 * K_LOADS)
            pe.wait_ge(wprep, 1)
            int_ffn(0)
            pe.wait_ge(w_in, 16 * W_LOADS)
            for b in range(B):
                pe.wait_ge(norm_ready, B * 1 + b + 1)
                turn_half(("turn", 1, b), lambda t: D[:, b, t], id_s[:])
            for b in range(B):
                for half in range(2):
                    key = ("qkv", b, half)
                    b0 = unit(key)
                    pe.wait_ge(act_unit, read_by("A", UNIT_AT[("turn", 1, b)]))
                    for q in range(4):
                        t = 4 * half + q
                        ins = te.matmul(ps[:, b0 + q, 0:3 * P], XT[:, b, t * P:(t + 1) * P], wkqv_s[:],
                                        start=True, stop=True)
                    ins.then_inc(pe_unit, 1)

            def free_slot(turn, k, i):
                for e, count in turn.freed(k, i):
                    pe.wait_ge(ring_read[e], count)
                return banks(turn.bank(k), 2)

            def scores(slot, off, lhsT, rhs, w, mask, mask_at):
                for c in range(0, w, 512):
                    n = min(512, w - c)
                    diag = c <= mask_at < c + n
                    ins = te.matmul(slot[:, off + c:off + c + n], lhsT, rhs[:, c:c + n], start=True, stop=not diag)
                    if diag:
                        ins = te.matmul(slot[:, off + mask_at:off + mask_at + P], idb_s[:], mask[:],
                                        start=False, stop=True)
                return ins

            def group_turn(turn, i, base, par):
                done = 0
                waiting = None

                def weigh(t, read):
                    gcount = base + done
                    pe.wait_ge(ring_act, read)
                    if t == 0:
                        pe.wait_ge(acc0_saved, gcount + START)
                        pe.wait_ge(v_staged, gcount + 1)
                    q0 = t * P
                    for bank in range(2):
                        a0, a1 = max(q0, 512 * bank), 512 * (bank + 1)
                        if a0 >= a1:
                            continue
                        for j in range(GH):
                            ins = te.matmul(ps[32 * j:32 * j + 32, 6 + bank, a0 - 512 * bank:512],
                                            VS[(par + done) % SETS][:, t, j], Pr[:, t % 2, j, a0 - q0:a1 - q0],
                                            start=t == 0, stop=t == 4 * bank + 3, tile_position=(0, 32 * j))
                    ins.then_inc(pv0, 1)

                for k, (kind, ahead, arg, reader) in enumerate(turn.steps):
                    g = base + done + ahead
                    r = (par + done + ahead) % SETS
                    if kind == "exp" and arg[:2] == (0, 0):
                        last = [q for q in range(k) if turn.steps[q][0] == "shifted_q"]
                        if last:
                            pe.wait_ge(ring_dve, turn.read("V", last[-1], i))
                        else:
                            pe.wait_ge(ring_dve, turn.c0["V"] + i * turn.reads("V"))
                    if kind == "max" and arg[:2] == (0, 0):
                        last = [q for q in range(k) if turn.steps[q][0] == "q"]
                        for e in "AV":
                            if last:
                                pe.wait_ge(ring_read[e], turn.read(e, last[-1], i))
                            else:
                                pe.wait_ge(ring_read[e], turn.c0[e] + i * turn.reads(e))
                    if kind == "heads":
                        pe.wait_ge(acc0_saved, base + done + 1 + START)
                    if kind == "shifted_q":
                        pe.wait_ge(shift_ready, g + 1)
                    slot = free_slot(turn, k, i)
                    if kind == "max":
                        t, j, n = arg
                        for q in range(n):
                            ins = scores(slot, q * (1024 // n), QT[:, (j + q) // 2, t * P:(t + 1) * P],
                                         KT[r][:, j + q], (t + 1) * P, mq_s, t * P)
                    if kind == "exp":
                        t, j, n = arg
                        for q in range(n):
                            ins = scores(slot, q * (1024 // n), KT[r][:, j + q, t * P:(t + 1) * P],
                                         QmT[r][:, (j + q) // 2, t * P:], (T - t) * P, mk_s, 0)
                    if kind in ("k", "q", "shifted_q"):
                        te.sem_inc(pe_gate, 1)
                        src = Ks if kind == "k" else Qs
                        dst = slot.bitcast(BF16)
                        for pair in (arg,) if kind == "k" else range(2):
                            for t in range(T):
                                c = (0 if kind == "k" else pair * S) + t * P
                                rows = src[:, bass.ds(2 * g + pair, 1), t].rearrange("p n s c -> p (n s c)")
                                ins = te.transpose(dst[:, c:c + P], rows, idb_s[:])
                    if kind == "heads":
                        for t in range(T):
                            ins = te.transpose(slot[:, t * P:(t + 1) * P], OT[:, t * P:(t + 1) * P], id_s[:])
                    ins.then_inc(ring_filled, 1)
                    nxt = turn.steps[k + 1][0] if k + 1 < len(turn.steps) else None
                    if waiting and (kind in ("exp", "shifted_q") or nxt == "heads"):
                        weigh(*waiting)
                        waiting = None
                    if kind == "exp" and arg[1] + arg[2] == GH:
                        waiting = (arg[0], turn.read("A", k, i))
                        if nxt == "heads":
                            weigh(*waiting)
                            waiting = None
                    if kind == "heads":
                        done += 1

            for n in range(2):
                u = UNIT_AT[("qkv", B - 1, 1)] - n
                pe.wait_ge(act_unit, read_by("A", u))
                pe.wait_ge(dve_unit, read_by("V", u))
            pe.wait_ge(dups_done, 2 * B)
            pe.wait_ge(slots_set, 2)
            group_turn(GROUP_FIRST, 0, 0, 0)
            with pe.Fori(0, GROUP_LOOP.times) as i:
                group_turn(GROUP_LOOP, i, SETS * i, 0)
            group_turn(GROUP_LAST, 0, G - 2, 0)

            for b in range(B):
                pe.wait_ge(acts_laid, b + 1)
                turn_half(("acts", b), lambda t: D[:, b, t], id_s[:], ring=GROUP_LAST)
            b0 = unit(("wscale",))
            pe.wait_ge(wmax_ready, 1)
            te.matmul(ps[:, b0, 0:2], ones_s[:], wmax[:], start=True, stop=True).then_inc(pe_unit, 1)
            for b in range(B):
                b0 = unit(("mm", 1, b))
                pe.wait_ge(act_unit, read_by("A", UNIT_AT[("acts", b)]))
                for t in range(T):
                    ins = te.matmul(banks(b0, 2)[:, t * P:(t + 1) * P], XT[:, b, t * P:(t + 1) * P], wo0_s[:],
                                    start=True, stop=True)
                ins.then_inc(pe_unit, 1)
            int_ffn(2)
            pe.wait_ge(wprep, 2)
            gated(3)
            for b in range(B):
                pe.wait_ge(norm_ready, B * 4 + b + 1)
                turn_half(("turn", 4, b), lambda t: D[:, b, t], id_s[:])

            def pair_turn(turn, i, first, start):
                done = 0
                waiting = None

                def weigh(t, read, r, pair):
                    pe.wait_ge(ring_act, read)
                    if t == 0:
                        pe.wait_ge(acc1_saved, pair + START)
                    q0 = t * P
                    src = Pr1[(t - 1) % 3] if t else Psum[r]
                    for bank in range(2):
                        a0, a1 = max(q0, 512 * bank), 512 * (bank + 1)
                        if a0 >= a1:
                            continue
                        for h in range(2):
                            ins = te.matmul(ps[h * D1:(h + 1) * D1, 6 + bank, a0 - 512 * bank:512],
                                            V1[r][:, t, h * D1:(h + 1) * D1], src[:, h, a0 - q0:a1 - q0],
                                            start=t == 0, stop=t == 4 * bank + 3, tile_position=(0, h * D1))
                    ins.then_inc(pv1, 1)

                def read_before(e, k, kinds):
                    last = [q for q in range(k) if turn.steps[q][0] in kinds]
                    if last:
                        pe.wait_ge(ring_read[e], turn.read(e, last[-1], i))
                    else:
                        pe.wait_ge(ring_read[e], turn.c0[e] + i * turn.reads(e))

                def products(kind, r, h, t, slot, off):
                    c0, w = (0, (t + 1) * P) if kind == "max" else (t * P, (T - t) * P)
                    at = t * P if kind == "max" else 0
                    for c in range(0, w, 512):
                        n = min(512, w - c)
                        diag = c <= at < c + n
                        tile, cols = slice(t * P, (t + 1) * P), slice(c0 + c, c0 + c + n)
                        if kind == "max":
                            ins = te.matmul(slot[:, off + c:off + c + n], Q1[r][:, h, tile], K1[r][:, h, cols],
                                            start=True, stop=not diag)
                        else:
                            te.matmul(slot[:, off + c:off + c + n], K1[r][:, h, tile], Q1[r][:, h, cols],
                                      start=True, stop=False)
                            ins = te.matmul(slot[:, off + c:off + c + n], K2[r][:, h, tile], Q2[r][:, h, cols],
                                            start=False, stop=not diag)
                        if diag:
                            ins = te.matmul(slot[:, off + at:off + at + P], idb_s[:], (mq_s if kind == "max" else mk_s)[:],
                                            start=False, stop=True)
                    return ins

                for k, (kind, h, arg, reader) in enumerate(turn.steps):
                    here = (first + done) % SETS
                    whole = first + start + done
                    if kind == "max" and arg[:2] == (0, 0):
                        pe.wait_ge(low_done, 4 * (whole + 1) + 2)
                        pe.wait_ge(copy_done, 2 * (whole + 1) + 2)
                    if kind == "shift":
                        pe.wait_ge(shift1_ready, whole + 2)
                    if kind == "exp" and arg[:2] == (0, 0):
                        read_before("A", k, ("shift",))
                        pe.wait_ge(low_done, 4 * whole + 4)
                    if kind == "proj_q":
                        pe.wait_ge(w_staged, whole + h + 1)
                    if kind == "sums":
                        pe.wait_ge(summed, (T - 1) * (whole + 1) + START)
                    if kind == "wo":
                        pe.wait_ge(y_done, whole - 1 + START)
                    slot = free_slot(turn, k, i)
                    if kind in ("max", "exp"):
                        t, j, n = arg
                        for q in range(n):
                            ins = products(kind, (here + h) % SETS, j + q, t, slot, q * (1024 // n))
                    if kind == "shift":
                        te.sem_inc(pe_gate, 1)
                        for q in range(T):
                            ins = te.transpose(slot.bitcast(F16)[D1:D1 + 2, q * P:(q + 1) * P], sh1[:, h, q],
                                               idh_s[:])
                    if kind in ("proj_q", "proj_k"):
                        for n in range(2):
                            ins = te.matmul(slot[:, 512 * n:512 * n + 512], ws1[:, (here + h) % SETS, int(kind == "proj_k")],
                                            XT[:, (first + done + h) // NP, 512 * n:512 * n + 512], start=True, stop=True)
                    if kind == "proj_v":
                        b, n = divmod(first + done + h, NP)
                        for q in range(T):
                            ins = te.matmul(slot[:, q * P:(q + 1) * P], XT[:, b, q * P:(q + 1) * P],
                                            wqkv1[:, 2, bass.ds((n + start) * P, P)], start=True, stop=True)
                    if kind == "sums":
                        for n in range(2):
                            for q in range(2):
                                ins = te.matmul(slot[q * D1:(q + 1) * D1, 512 * n:512 * n + 512],
                                                ones_s[:, q * D1:(q + 1) * D1], Psum[here][:, q, 512 * n:512 * n + 512],
                                                start=True, stop=True, tile_position=(0, q * D1))
                    if kind == "wo":
                        for n in range(NP):
                            if n == NP - 1:
                                pe.wait_ge(y_done, whole + START)
                            for t in range(T):
                                ins = te.matmul(slot[:, t * P:(t + 1) * P], YT[:, n, t * P:(t + 1) * P],
                                                wo1_s[:, n], start=n == 0 and t % 4 == 0, stop=n == NP - 1,
                                                skip_group_check=True)
                    ins.then_inc(ring_filled, 1)
                    after = turn.steps[k + 1][0] if k + 1 < len(turn.steps) else None
                    if waiting and (kind == "exp" or waiting[0] == T - 1):
                        weigh(*waiting)
                        waiting = None
                    if kind == "exp" and arg[1] + arg[2] == 2:
                        waiting = (arg[0], turn.read("A", k, i), here, whole)
                        if after == "sums":
                            weigh(*waiting)
                            waiting = None
                    if kind == "sums":
                        done += 1

            for n in range(2):
                pe.wait_ge(act_unit, read_by("A", UNIT_AT[("turn", 4, B - 1)] - n))
            pair_turn(PAIR_FIRST, 0, -1, 0)
            pe.wait_ge(rows_set, 3 * SETS)
            for b, (loop, last) in enumerate(PAIR_TURNS):
                with pe.Fori(0, loop.times) as i:
                    pair_turn(loop, i, b * NP, SETS * i)
                pair_turn(last, 0, (b + 1) * NP - 2, 0)
            gated(5)


def _constants():
    import numpy as np

    eye = np.eye(P, dtype=np.float32)
    row, col = np.arange(P)[:, None], np.arange(P)[None, :]
    inv_freq = np.float32(1.0) / np.float32(10000.0) ** (np.arange(0, D0, 2, dtype=np.float32) / np.float32(D0))
    ang = np.arange(S, dtype=np.float32)[:, None] * inv_freq[None, :]
    cos = np.tile(np.repeat(np.cos(ang), 2, axis=1), (1, 2 * H))
    sin = np.repeat(np.sin(ang), 2, axis=1)
    sin[:, 0::2] *= -1
    sin = np.tile(sin, (1, 2 * H))
    by_tile = lambda a: np.ascontiguousarray(a.reshape(T, P, -1).transpose(1, 0, 2)).astype(np.float32)
    hh = (np.arange(P) // D0) % 2
    return {
        "ident": eye,
        "mask_q": np.where(col > row, np.float32(-1e30), np.float32(0)),
        "mask_k": np.where(col < row, np.float32(-1e30), np.float32(0)),
        "head_mask": np.stack([hh == 0, hh == 1], axis=1).astype(np.float32),
        "rope_cos": by_tile(cos),
        "rope_sin": by_tile(sin),
    }


def kernel(L0_attn_X, L0_attn_W_KQV, L0_attn_W_O, L0_ffn_weight_q, L0_ffn_weight_scale, L0_ffn_bias,
           L1_attn_w_q, L1_attn_w_k, L1_attn_w_v, L1_attn_w_o, L1_ffn_w_gate, L1_ffn_w_up, L1_ffn_w_down):
    import numpy as np
    import concourse.bacc as bacc
    from concourse.bass_utils import run_bass_kernel_spmd

    def lay(a):
        return np.ascontiguousarray(a)

    arrays = {
        "x": lay(L0_attn_X).reshape(B * S, P),
        "w_kqv": lay(np.asarray(L0_attn_W_KQV).T),
        "w_o0": lay(np.asarray(L0_attn_W_O).T),
        "w_int": lay(np.asarray(L0_ffn_weight_q).T).astype(np.int64),
        "w_scale": lay(np.broadcast_to(np.asarray(L0_ffn_weight_scale), (P, P))),
        "bias": lay(np.broadcast_to(np.asarray(L0_ffn_bias), (P, P))),
        "w_q": lay(np.asarray(L1_attn_w_q).reshape(H * D1, P).T),
        "w_k": lay(np.asarray(L1_attn_w_k).reshape(H * D1, P).T),
        "w_v": lay(np.asarray(L1_attn_w_v).reshape(H * D1, P).T),
        "w_o1": lay(L1_attn_w_o),
        "w_gate": lay(np.asarray(L1_ffn_w_gate).T),
        "w_up": lay(np.asarray(L1_ffn_w_up).T),
        "w_down": lay(np.asarray(L1_ffn_w_down).T),
    }
    arrays.update(_constants())
    nc = bacc.Bacc("TRN2", target_bir_lowering=False, num_devices=1)
    args = [nc.dram_tensor(f"in_{n}_dram", a.shape, mybir.dt.from_np(a.dtype), kind="ExternalInput").ap()
            for n, a in arrays.items()]
    args.append(nc.dram_tensor("out_0_dram", (B * S, P), F32, kind="ExternalOutput").ap())
    macaron_block_kernel(nc, *args)
    r = run_bass_kernel_spmd(nc, [{f"in_{n}_dram": a for n, a in arrays.items()}], core_ids=[0])
    return r.results[0]["out_0_dram"].reshape(B, S, P)
```
